# Optimizing a Trainium2 kernel written in Bass

```python
import numpy as np
import jax
import jax.numpy as jnp

def _softmax(x, axis=-1):
    return jax.nn.softmax(x, axis=axis)

def _gelu(x):
    return jax.nn.gelu(x, approximate=True)

def _silu(x):
    return jax.nn.silu(x)

def _sigmoid(x):
    return jax.nn.sigmoid(x)

def _layernorm(x, axis=-1, eps=1e-05):
    m = jnp.mean(x, axis=axis, keepdims=True)
    v = jnp.var(x, axis=axis, keepdims=True)
    return (x - m) / jnp.sqrt(v + eps)

def _scatter_add(tgt, idx, src, axis=0):
    return tgt.at[idx].add(src)

def _segment_sum(src, seg, n):
    return jax.ops.segment_sum(src, seg, n)
kernel_name = 'mk_macaron_d1_jaxref_r8_c410d8'

def setup_inputs(seed: int=0):
    np.random.seed(seed)
    _w = jnp.asarray

    def _L0_attn_setup():
        import jax, jax.numpy as jnp
        import numpy as np
        D_MODEL = 256
        GN_EPS = 1e-05
        key = jax.random.key(seed)
        ks = jax.random.split(key, 6)
        B, T, D = (4, 256, D_MODEL)
        s = 1.0 / np.sqrt(D)
        return {'x': jax.random.normal(ks[0], (B, T, D), dtype=jnp.float32), 'Wr': jax.random.normal(ks[1], (D, D), dtype=jnp.float32) * s, 'Wk': jax.random.normal(ks[2], (D, D), dtype=jnp.float32) * s, 'Wv': jax.random.normal(ks[3], (D, D), dtype=jnp.float32) * s, 'Wo': jax.random.normal(ks[4], (D, D), dtype=jnp.float32) * s, 'decay': jnp.ones((D,), dtype=jnp.float32) * 0.99, 'gn_weight': jnp.ones((D,), dtype=jnp.float32), 'gn_bias': jnp.zeros((D,), dtype=jnp.float32)}
    _L0_attn_in = _L0_attn_setup()

    def _L0_ffn_setup():
        import jax, jax.numpy as jnp
        import numpy as np
        from jax import lax
        B, S, H = (1, 256, 256)
        E, I, TOP_K = (64, 64, 8)
        SHARED_I = 64
        key = jax.random.key(seed)
        ks = jax.random.split(key, 8)
        sc = 0.02
        return {'hidden_states': jax.random.normal(ks[0], (B, S, H), jnp.float32), 'router_w': jax.random.normal(ks[1], (E, H), jnp.float32) * sc, 'gate_up_proj': jax.random.normal(ks[2], (E, 2 * I, H), jnp.float32) * sc, 'down_proj': jax.random.normal(ks[3], (E, H, I), jnp.float32) * sc, 'shared_gate_w': jax.random.normal(ks[4], (SHARED_I, H), jnp.float32) * sc, 'shared_up_w': jax.random.normal(ks[5], (SHARED_I, H), jnp.float32) * sc, 'shared_down_w': jax.random.normal(ks[6], (H, SHARED_I), jnp.float32) * sc, 'shared_expert_gate_w': jax.random.normal(ks[7], (1, H), jnp.float32) * sc}
    _L0_ffn_in = _L0_ffn_setup()
    _d = {'L0_attn_x': _L0_attn_in['x'], 'L0_attn_Wr': _L0_attn_in['Wr'], 'L0_attn_Wk': _L0_attn_in['Wk'], 'L0_attn_Wv': _L0_attn_in['Wv'], 'L0_attn_Wo': _L0_attn_in['Wo'], 'L0_attn_decay': _L0_attn_in['decay'], 'L0_attn_gn_weight': _L0_attn_in['gn_weight'], 'L0_attn_gn_bias': _L0_attn_in['gn_bias'], 'L0_ffn_router_w': _L0_ffn_in['router_w'], 'L0_ffn_gate_up_proj': _L0_ffn_in['gate_up_proj'], 'L0_ffn_down_proj': _L0_ffn_in['down_proj'], 'L0_ffn_shared_gate_w': _L0_ffn_in['shared_gate_w'], 'L0_ffn_shared_up_w': _L0_ffn_in['shared_up_w'], 'L0_ffn_shared_down_w': _L0_ffn_in['shared_down_w'], 'L0_ffn_shared_expert_gate_w': _L0_ffn_in['shared_expert_gate_w']}
    _x0 = _d['L0_attn_x']
    _d['L0_attn_x'] = jax.random.normal(jax.random.fold_in(jax.random.key(seed), 1), (4, 1024, 256), dtype=_x0.dtype)
    del _x0
    return _d

def reference(L0_attn_x, L0_attn_Wr, L0_attn_Wk, L0_attn_Wv, L0_attn_Wo, L0_attn_decay, L0_attn_gn_weight, L0_attn_gn_bias, L0_ffn_router_w, L0_ffn_gate_up_proj, L0_ffn_down_proj, L0_ffn_shared_gate_w, L0_ffn_shared_up_w, L0_ffn_shared_down_w, L0_ffn_shared_expert_gate_w):

    def _L0_attn_ref(x, Wr, Wk, Wv, Wo, decay, gn_weight, gn_bias):
        import jax, jax.numpy as jnp
        import numpy as np
        D_MODEL = 256
        GN_EPS = 1e-05
        B, T, D = x.shape
        r = jax.nn.sigmoid(jnp.einsum('btd,ed->bte', x, Wr))
        k = jnp.einsum('btd,ed->bte', x, Wk)
        v = jnp.einsum('btd,ed->bte', x, Wv)
        d = jax.nn.sigmoid(decay)
        log_decay = jnp.log(jnp.clip(d, 1e-07, None))
        pos = jnp.arange(T, dtype=x.dtype)
        scale = jnp.exp(pos[:, None] * log_decay[None, :])
        scaled = k * v / jnp.clip(scale, 1e-10, None)[None]
        state = jnp.cumsum(scaled, axis=1) * scale[None]
        out = r * state
        mean = jnp.mean(out, axis=(1, 2), keepdims=True)
        var = jnp.mean(jnp.square(out - mean), axis=(1, 2), keepdims=True)
        normed = (out - mean) * jax.lax.rsqrt(var + GN_EPS)
        normed = normed * gn_weight + gn_bias
        return jnp.einsum('btd,ed->bte', normed, Wo)

    def _L0_ffn_ref(hidden_states, router_w, gate_up_proj, down_proj, shared_gate_w, shared_up_w, shared_down_w, shared_expert_gate_w):
        import jax, jax.numpy as jnp
        import numpy as np
        from jax import lax
        B, S, H = (1, 256, 256)
        E, I, TOP_K = (64, 64, 8)
        SHARED_I = 64
        b, s, h_dim = hidden_states.shape
        h = hidden_states.reshape(-1, h_dim)
        T = h.shape[0]
        shared = jnp.dot(jax.nn.silu(jnp.dot(h, shared_gate_w.T)) * jnp.dot(h, shared_up_w.T), shared_down_w.T)
        shared = jax.nn.sigmoid(jnp.dot(h, shared_expert_gate_w.T)) * shared
        logits = jnp.dot(h, router_w.T)
        probs = jax.nn.softmax(logits.astype(jnp.float32), axis=-1)
        top_vals, top_idx = lax.top_k(probs, TOP_K)
        top_vals = top_vals / jnp.sum(top_vals, axis=-1, keepdims=True)
        top_vals = top_vals.astype(h.dtype)
        comb = jnp.zeros((T, E), h.dtype).at[jnp.arange(T)[:, None], top_idx].add(top_vals)

        def body(acc, xs):
            wgu, wd, w_e = xs
            g, u = jnp.split(jnp.dot(h, wgu.T), 2, axis=-1)
            eo = jnp.dot(jax.nn.silu(g) * u, wd.T)
            return (acc + eo * w_e[:, None], None)
        expert_out, _ = lax.scan(body, jnp.zeros_like(h), (gate_up_proj, down_proj, comb.T))
        return (expert_out + shared).reshape(b, s, h_dim)
    x = L0_attn_x
    x = x + 0.5 * _L0_ffn_ref(_layernorm(x, axis=-1), L0_ffn_router_w, L0_ffn_gate_up_proj, L0_ffn_down_proj, L0_ffn_shared_gate_w, L0_ffn_shared_up_w, L0_ffn_shared_down_w, L0_ffn_shared_expert_gate_w)
    x = x + _L0_attn_ref(_layernorm(x, axis=-1), L0_attn_Wr, L0_attn_Wk, L0_attn_Wv, L0_attn_Wo, L0_attn_decay, L0_attn_gn_weight, L0_attn_gn_bias)
    x = x + 0.5 * _L0_ffn_ref(_layernorm(x, axis=-1), L0_ffn_router_w, L0_ffn_gate_up_proj, L0_ffn_down_proj, L0_ffn_shared_gate_w, L0_ffn_shared_up_w, L0_ffn_shared_down_w, L0_ffn_shared_expert_gate_w)
    return x

_drawn_inputs = setup_inputs


def setup_inputs(seed=0):
    import zlib

    import numpy as np

    out = dict(_drawn_inputs(seed))
    spreads = {'L0_attn_decay': (0.9900000095367432, 0.2),
     'L0_attn_gn_weight': (1.0, 0.2),
     'L0_attn_gn_bias': (0.0, 0.1)}
    factors = {'L0_ffn_router_w': 8.0,
     'L0_ffn_gate_up_proj': 8.0,
     'L0_ffn_down_proj': 8.0,
     'L0_ffn_shared_gate_w': 8.0,
     'L0_ffn_shared_up_w': 8.0,
     'L0_ffn_shared_down_w': 8.0,
     'L0_ffn_shared_expert_gate_w': 8.0}
    for name, (base, spread) in spreads.items():
        noise = np.random.default_rng([zlib.crc32(name.encode()), seed]).standard_normal(out[name].shape)
        drawn = base * np.exp(spread * noise) if base else spread * noise
        out[name] = jnp.asarray(drawn.astype(out[name].dtype))
    for name, factor in factors.items():
        out[name] = (out[name] * factor).astype(out[name].dtype)
    return out
```

```python
from contextlib import ExitStack, contextmanager

import concourse.bass as bass
from concourse import mybir

F32 = mybir.dt.float32
F32R = mybir.dt.float32r
ALU = mybir.AluOpType
ACT = mybir.ActivationFunctionType
AX_X = mybir.AxisListType.X

P = 128
D = 256
KC = D // P
B, T = 4, 1024
TILES = T // P
CH = 512
CHUNKS = T // CH
E, I, TOPK = 64, 64, 8
COLS = E + 1
PAIRS = E // 2 + 1
SLOTS = 3
STEPS = PAIRS // SLOTS
PAIR_W = 4 * P + D
SEAM = STEPS - 1
ROUTE = TILES
EPS = 1e-5
GOLD = 16
FIRST_PRODUCTS = ((0, 0), (0, 1), (1, 0))
assert PAIRS == STEPS * SLOTS and ROUTE < SEAM

SPLIT_CREDIT = SLOTS
DOWN_CREDIT = 4
WEIGHTED_CREDIT = 2 * SLOTS
HIDDEN_CREDIT = 2
ONE = 1
PROJ_CREDIT = 2


class Count:

    def __init__(self, start=0):
        self.base, self.off = start, 0

    def at(self, more=0):
        return self.base + (self.off + more) if self.off + more else self.base

    def up(self):
        self.off += 1
        return self.at()


@contextmanager
def counted_loop(eng, times, counts, per):
    before = [(c.base, c.off) for c in counts]
    with eng.Fori(0, times) as i:
        for c, (base, off), k in zip(counts, before, per):
            c.base, c.off = base + i * k + off, 0
        yield i
        for c, k in zip(counts, per):
            assert c.off == k, (c.off, k)
    for c, (base, off), k in zip(counts, before, per):
        c.base, c.off = base, off + times * k


def build(nc, x, w_pairs, w_router, w_attn, decay, gn, eye, pos, out):
    with ExitStack() as ctx:
        def sb(name, shape, dt=F32):
            return ctx.enter_context(nc.sbuf_tensor(name, shape, dt))

        def bank(name):
            return ctx.enter_context(nc.psum_tensor(name, [P, CH], F32))

        def sem(name):
            return ctx.enter_context(nc.semaphore(name))

        X = sb("X", [P, B * TILES, D])
        raw_w = sb("raw_w", [P, SLOTS, PAIR_W])
        hi_w = sb("hi_w", [P, SLOTS, PAIR_W], F32R)
        lo_w = sb("lo_w", [P, SLOTS, PAIR_W], F32R)
        hi_z = sb("hi_z", [P, 2, KC, T], F32R)
        lo_z = sb("lo_z", [P, 2, KC, T], F32R)
        weight_b = sb("weight_b", [P, SLOTS, T])
        hid = sb("hid", [P, 2, CH])
        hi_h = sb("hi_h", [P, 2, CH], F32R)
        lo_h = sb("lo_h", [P, 2, CH], F32R)
        ffn_o = sb("ffn_o", [P, KC, T])
        z = sb("z", [P, D])
        zt = sb("zt", [P, KC, P])
        bn6 = sb("bn6", [P, 6])
        relay = sb("relay", [P, 1])
        mv = sb("mv", [P, 2])
        mean = sb("mean", [P, TILES])
        ve = sb("ve", [P, TILES])
        rstd = sb("rstd", [P, TILES])
        mhalf = sb("mhalf", [P, TILES])
        logit = sb("logit", [P, TILES, COLS])
        row_max = sb("row_max", [P, TILES])
        ex = sb("ex", [P, TILES, COLS])
        top = sb("top", [P, TILES, TOPK])
        rest = sb("rest", [P, TILES, E])
        tot = sb("tot", [P, TILES])
        rtot = sb("rtot", [P, TILES])
        comb = sb("comb", [P, TILES, COLS])
        comb_t = sb("comb_t", [COLS, T])
        ident = sb("ident", [P, P])
        router = sb("router", [P, KC, COLS])
        hi_a = sb("hi_a", [P, 4, KC, D], F32R)
        lo_a = sb("lo_a", [P, 4, KC, D], F32R)
        r_s = sb("r_s", [P, KC, T])
        k_s = hid
        state = sb("state", [P, KC, T])
        scale = sb("scale", [P, KC, T])
        inv = sb("inv", [P, KC, T])
        hi_n = sb("hi_n", [P, KC, T], F32R)
        lo_n = sb("lo_n", [P, KC, T], F32R)
        ones = sb("ones", [P, 1])
        mean_w = sb("mean_w", [P, P])
        par = sb("par", [P, 3, KC])
        bn24 = sb("bn24", [P, 4, 6])
        gstat = sb("gstat", [P, 8])
        aff = sb("aff", [P, 2, KC])

        O = [[bank(f"O{m}{c}") for c in range(CHUNKS)] for m in range(KC)]
        G, U, S0, S1 = bank("G"), bank("U"), bank("S0"), bank("S1")
        comb_d = nc.dram_tensor("comb_scratch", (2, COLS, T), F32).ap()
        raw_a = state[:, :, :].rearrange("p k t -> p (k t)")
        pos_b = r_s[:, 0, :]

        x_in = [sem(f"x_in{b}") for b in range(B)]
        consts_in = [sem(f"consts_in{i}") for i in range(7)]
        w_in = [sem(f"w_in{i}") for i in range(SLOTS)]
        weight_in = [sem(f"weight_in{i}") for i in range(SLOTS)]
        w_hi, w_split = sem("w_hi"), sem("w_split")
        gate_done, up_done, down_done = sem("gate_done"), sem("up_done"), sem("down_done")
        silu_done, gated, weighted, hid_hi, hidden = (sem(n) for n in ("silu_done", "gated", "weighted", "hid_hi", "hidden"))
        out0_done, out1_done = sem("out0_done"), sem("out1_done")
        s0_full, s0_used, s1_full, s1_used = (sem(n) for n in ("s0_full", "s0_used", "s1_full", "s1_used"))
        mean_done = sem("mean_done")
        var_done, rstd_done, z_done, z_hi = sem("var_done"), sem("rstd_done"), sem("z_done"), sem("z_hi")
        ex_in, ex_done, comb_done, comb_out = (sem(n) for n in ("ex_in", "ex_done", "comb_done", "comb_out"))
        dve_link, act_link = sem("dve_link"), sem("act_link")
        mem_set, exponent_set = sem("mem_set"), sem("exponent_set")
        k_full, v_full, r_full = sem("k_full"), sem("v_full"), sem("r_full")
        k_copied, k_scaled, kv_done, r_copied, r_scaled = (sem(n) for n in ("k_copied", "k_scaled", "kv_done", "r_copied", "r_scaled"))
        part_done, avg_done, group_var, group_rstd, spread_done, affine, normed, n_split, wo_done, added = (
            sem(n) for n in ("part_done", "avg_done", "group_var", "group_rstd", "spread_done", "affine", "normed", "n_split", "wo_done", "added"))
        a_hi, a_lo, table_done, table_in, decay_done = sem("a_hi"), sem("a_lo"), sem("table_done"), sem("table_in"), sem("decay_done")
        stored = sem("stored")

        PREP = TILES + 1
        PASS_USES = PREP + (B - 1) * (PREP + 2) + 2
        S0_AT = [ONE, ONE + PASS_USES + B * TILES]
        S1_AT = [ONE, ONE + PASS_USES]
        S0_ATT = ONE + PASS_USES
        UNITS = 2 * SLOTS

        def walk_pass(eng, ps, prepare, block):
            prepare(ps)
            with eng.Fori(0, B - 1) as b:
                block(ps, b, False)
            block(ps, B - 1, True)

        blk = nc.Block()
        block_ctx = ctx.enter_context(blk)

        @block_ctx.sync
        def _(sp):
            sp.dma_start(X[:, 0:TILES, :], x[0].rearrange("(t p) c -> p t c", p=P)).then_inc(x_in[0], GOLD)
            sp.dma_start(ident[:], eye).then_inc(consts_in[0], GOLD)
            sp.dma_start(router[:], w_router).then_inc(consts_in[1], GOLD)
            for b in range(1, B):
                sp.dma_start(X[:, b * TILES:(b + 1) * TILES, :],
                             x[b].rearrange("(t p) c -> p t c", p=P)).then_inc(x_in[b], GOLD)

            def load_w(pair, n, p):
                sp.wait_ge(w_split, n + 1)
                sp.dma_start(raw_w[:, p, :], w_pairs[pair]).then_inc(w_in[p], GOLD)

            def step(ps, b, j, seam=False, final=False):
                s = (ps * B + b) * STEPS + j
                for p in range(SLOTS):
                    n = s * SLOTS + p
                    if not (seam and p > 0):
                        load_w(j * SLOTS + p + 2, n + 2, (p + 2) % SLOTS)
                    elif not final:
                        load_w(p - 1, n + 2, p - 1)
                    if p == 0 and isinstance(j, int) and j == 0:
                        sp.wait_ge(comb_out, GOLD * (ps * B + b + 1))
                    sp.wait_ge(weighted, 2 * n + 2)
                    par_b = (ps * B + b) % 2
                    for half in range(2):
                        e = E if (seam and p == SLOTS - 1) else (j * SLOTS + p) * 2 + half
                        sp.dma_start(weight_b[half * I:(half + 1) * I, p, :],
                                     comb_d[bass.ds(par_b, 1), bass.ds(e, 1), :].rearrange("o e t -> (o e) t").to_broadcast([I, T])).then_inc(weight_in[p], GOLD)

            def block(ps, b, last):
                step(ps, b, 0)
                with sp.Fori(1, SEAM) as j:
                    step(ps, b, j)
                step(ps, b, SEAM, True, last and ps == 1)

            load_w(0, 0, 0)
            load_w(1, 1, 1)
            sp.dma_start(raw_a, w_attn).then_inc(consts_in[2], GOLD)
            sp.dma_start(pos_b, pos.to_broadcast([P, T])).then_inc(consts_in[3], GOLD)
            sp.dma_start(par[:, 0, :], decay).then_inc(consts_in[4], GOLD)
            sp.dma_start(par[:, 1:3, :], gn).then_inc(consts_in[5], GOLD)
            for ps in range(2):
                walk_pass(sp, ps, lambda ps: None, block)

        @block_ctx.gpsimd
        def _(pool):
            pool.sem_inc(w_split, SPLIT_CREDIT)
            pool.sem_inc(down_done, DOWN_CREDIT)
            pool.sem_inc(weighted, WEIGHTED_CREDIT)
            pool.sem_inc(hidden, HIDDEN_CREDIT)
            pool.sem_inc(kv_done, PROJ_CREDIT)
            for guard in (s0_full, s0_used, s1_full, s1_used, out0_done, out1_done, part_done, added, wo_done):
                pool.sem_inc(guard, ONE)
            pool.memset(mhalf[:], -0.5).then_inc(exponent_set, 1)
            pool.wait_ge(exponent_set, 1)

            def rstd_of(j, n, tiles):
                tiles.off += n
                pool.wait_ge(var_done, tiles.at())
                pool.tensor_tensor(rstd[:, bass.ds(j, n)], ve[:, bass.ds(j, n)], mhalf[:, 0:n], ALU.pow).then_inc(rstd_done, 1)

            def split_lo(s, p):
                n = s * SLOTS + p
                pool.wait_ge(w_hi, n + 1)
                pool.tensor_tensor(lo_w[:, p, :], raw_w[:, p, :], hi_w[:, p, :].bitcast(F32),
                                   ALU.subtract).then_inc(w_split, 1)

            rst = Count()

            def split_ahead(s, p):
                split_lo(s + (p + 2) // SLOTS, (p + 2) % SLOTS)

            def prepare(ps):
                rstd_of(0, TILES, rst)

            def step(s, final=False):
                for p in range(SLOTS):
                    if not final or p + 2 < SLOTS:
                        split_ahead(s, p)

            def block(ps, b, last):
                s0 = (ps * B + b) * STEPS
                if not last:
                    with counted_loop(pool, TILES, [rst], [1]) as j:
                        rstd_of(j, 1, rst)
                        step(s0 + j)
                    for j in range(TILES, SEAM):
                        step(s0 + j)
                else:
                    with pool.Fori(0, SEAM) as j:
                        step(s0 + j)
                step(s0 + SEAM, final=last and ps == 1)
                if ps == 1:
                    pool.wait_ge(s0_used, uses_after(0, ps, b, last))
                    pool.wait_ge(s1_used, uses_after(1, ps, b, last))
                    pool.dma_start(out[bass.ds(b, 1), :, :].rearrange("o (t p) c -> p (o t) c", p=P),
                                   X[:, bass.ds(b * TILES, TILES), :]).then_inc(stored, GOLD)

            def uses_after(which, ps, b, last):
                at = (S0_AT if which == 0 else S1_AT)[ps] + PREP
                return at + (B - 1) * (PREP + 2) + 2 if last else at + (b + 1) * (PREP + 2)

            def pool_pass(ps):
                prepare(ps)
                with counted_loop(pool, B - 1, [rst], [TILES]) as b:
                    block(ps, b, False)
                block(ps, B - 1, True)

            split_lo(0, 0)
            split_lo(0, 1)
            pool_pass(0)

            with counted_loop(pool, B, [rst], [TILES]) as b:
                rstd_of(0, TILES, rst)
                for i in range(4):
                    c, m = divmod(i, KC)
                    q = b * 4 + i
                    pool.wait_ge(k_copied, q + 1)
                    if i == 0:
                        pool.wait_ge(table_done, 2 * KC)
                    pool.tensor_tensor(k_s[:, i % 2, :], k_s[:, i % 2, :], inv[:, m, c * CH:(c + 1) * CH],
                                       ALU.mult).then_inc(k_scaled, 1)
                    pool.wait_ge(r_copied, q + 1)
                    rs = r_s[:, m, c * CH:(c + 1) * CH]
                    pool.tensor_tensor(rs, rs, scale[:, m, c * CH:(c + 1) * CH], ALU.mult).then_inc(r_scaled, 1)
                pool.wait_ge(group_var, b + 1)
                pool.tensor_tensor(gstat[:, 6:7], gstat[:, 5:6], mhalf[:, 0:1], ALU.pow).then_inc(group_rstd, 1)

            pool_pass(1)
            pool.wait_ge(stored, B * GOLD)

        @block_ctx.scalar
        def _(act):
            zc = Count()
            ec = Count()

            def split_hi(s, p):
                n = s * SLOTS + p
                act.wait_ge(w_in[p], GOLD * (s + 1))
                act.wait_ge(down_done, 2 * n)
                nc.scalar.activation(hi_w[:, p, :], raw_w[:, p, :], ACT.Copy).then_inc(w_hi, 1)

            def silu(s, p, c):
                u = s * UNITS + 2 * p + c
                act.wait_ge(gate_done, u + 1)
                act.wait_ge(hidden, u + HIDDEN_CREDIT - 1)
                nc.scalar.activation(hid[:, c, :], G[:], ACT.Silu).then_inc(silu_done, 1)

            def high_z(zp, j, s0_at):
                act.wait_ge(s0_full, s0_at + 1)
                nc.scalar.activation(hi_z[:, zp, :, bass.ds(j * P, P)],
                                     S0[:, 0:D].rearrange("p (k t) -> p k t", k=KC), ACT.Copy).then_inc(z_hi, 1)

            def exps():
                k = ec.up()
                act.wait_ge(ex_in, k + k)
                nc.scalar.activation(ex[:], ex[:], ACT.Exp).then_inc(ex_done, 1)

            def store_comb(k, s0_at, s1_at):
                act.wait_ge(s0_used, s0_at + 1)
                act.wait_ge(s1_used, s1_at + 1)
                act.dma_start(comb_d[bass.ds(k % 2, 1)].rearrange("o e t -> (o e) t"), comb_t[:]).then_inc(comb_out, GOLD)

            def out_copy(k_block, c, s1_before):
                act.wait_ge(down_done, DOWN_CREDIT + 2 * PAIRS * (k_block + 1) - (1 - c))
                act.wait_ge(s1_full, s1_before)
                nc.scalar.activation(ffn_o[:, 0, c * CH:(c + 1) * CH], O[0][c][:], ACT.Copy, scale=0.5).then_inc(out0_done, 1)

            def step(s, final=False, side=None):
                for p in range(SLOTS):
                    silu(s, p, 0)
                    silu(s, p, 1)
                    if side and p == 1:
                        side()
                    if not final or p + 2 < SLOTS:
                        split_hi(s + (p + 2) // SLOTS, (p + 2) % SLOTS)

            def s1_before_seam(ps, b, last):
                at = S1_AT[ps] + PREP
                if last:
                    return at + (B - 1) * (PREP + 2)
                return at + b * (PREP + 2)

            def block(ps, b, last):
                k = ps * B + b
                s0 = k * STEPS
                if not last:
                    s0_at = S0_AT[ps] + PREP + b * (PREP + 2)
                    with act.Fori(0, TILES) as j:
                        step(s0 + j, side=lambda: high_z((b + 1) % 2, j, s0_at + j))
                    step(s0 + ROUTE, side=exps)
                    store_comb(k + 1, s0_at + TILES, S1_AT[ps] + PREP + b * (PREP + 2) + TILES)
                    for j in range(ROUTE + 1, SEAM):
                        step(s0 + j)
                else:
                    with act.Fori(0, SEAM) as j:
                        step(s0 + j)
                step(s0 + SEAM, final=last and ps == 1)
                for c in range(CHUNKS):
                    out_copy(k, c, s1_before_seam(ps, b, last))

            def prepare(ps):
                with act.Fori(0, TILES) as j:
                    high_z(0, j, S0_AT[ps] + j)
                exps()
                store_comb(0, S0_AT[ps] + TILES, S1_AT[ps] + TILES)

            def act_pass(ps):
                prepare(ps)
                with counted_loop(act, B - 1, [ec], [1]) as b:
                    block(ps, b, False)
                block(ps, B - 1, True)

            act.wait_ge(consts_in[4], GOLD)
            nc.scalar.activation(par[:, 0, :], par[:, 0, :], ACT.Sigmoid).then_inc(act_link, 1)
            act.wait_ge(decay_done, 1)
            nc.scalar.activation(par[:, 0, :], par[:, 0, :], ACT.Ln).then_inc(act_link, 1)
            act.wait_ge(act_link, 2)
            act.wait_ge(consts_in[3], GOLD)
            for m in range(KC):
                nc.scalar.activation(scale[:, m, :], pos_b, ACT.Exp, scale=par[:, 0, m:m + 1]).then_inc(table_in, 1)
            act.wait_ge(consts_in[2], GOLD)
            nc.scalar.activation(hi_a[:].rearrange("p w k n -> p (w k n)"), raw_a, ACT.Copy).then_inc(a_hi, 1)
            split_hi(0, 0)
            split_hi(0, 1)
            act_pass(0)

            with act.Fori(0, B) as b:
                with act.Fori(0, TILES) as j:
                    high_z(b % 2, j, S0_ATT + b * TILES + j)
                for i in range(4):
                    c, m = divmod(i, KC)
                    q = b * 4 + i
                    act.wait_ge(k_full, q + 1)
                    act.wait_ge(kv_done, q + 1)
                    nc.scalar.activation(k_s[:, i % 2, :], O[0][i % 2][:], ACT.Copy).then_inc(k_copied, 1)
                    act.wait_ge(r_full, q + 1)
                    if i == 0:
                        act.wait_ge(part_done, b + ONE)
                    nc.scalar.activation(r_s[:, m, c * CH:(c + 1) * CH], (G if i % 2 == 0 else U)[:],
                                         ACT.Sigmoid).then_inc(r_copied, 1)
                act.wait_ge(affine, b + 1)
                for m in range(KC):
                    nc.scalar.activation(state[:, m, :], state[:, m, :], ACT.Identity, bias=aff[:, 1, m:m + 1],
                                         scale=aff[:, 0, m:m + 1]).then_inc(normed, 1)
            act_pass(1)

        @block_ctx.vector
        def _(dve):
            link = Count()
            vc = Count()
            zc = Count()
            rc = Count()

            def linked(ins):
                ins.then_inc(dve_link, 1)
                dve.wait_ge(dve_link, link.up())

            def stats(t, j):
                linked(nc.vector.bn_stats(bn6[:], X[:, bass.ds(t, 1), :].rearrange("p o c -> p (o c)")))
                nc.vector.tensor_copy(relay[:], bn6[:, 0:1])
                linked(nc.vector.bn_aggr(mv[:], bn6[:]))
                nc.vector.tensor_copy(mean[:, bass.ds(j, 1)], mv[:, 0:1]).then_inc(mean_done, 1)
                nc.vector.tensor_scalar(ve[:, bass.ds(j, 1)], mv[:, 1:2], EPS, None, ALU.add).then_inc(var_done, 1)

            def normalise(t, j, s0_at):
                dve.wait_ge(rstd_done, vc.at())
                dve.wait_ge(s0_full, s0_at)
                zc.up()
                nc.vector.tensor_scalar(z[:], X[:, bass.ds(t, 1), :].rearrange("p o c -> p (o c)"),
                                        mean[:, bass.ds(j, 1)],
                                        rstd[:, bass.ds(j, 1)], ALU.subtract, ALU.mult).then_inc(z_done, 1)

            def low_z(zp, j, s0_at, s1_at):
                dve.wait_ge(z_hi, zc.at())
                src = S0[:, 0:D].rearrange("p (k t) -> p k t", k=KC)
                ins = nc.vector.tensor_tensor(lo_z[:, zp, :, bass.ds(j * P, P)], src,
                                              hi_z[:, zp, :, bass.ds(j * P, P)].bitcast(F32), ALU.subtract)
                if s1_at is None:
                    ins.then_inc(s0_used, 1)
                    return
                dve.wait_ge(s1_full, s1_at)
                nc.vector.tensor_copy(zt[:], src).then_inc(s0_used, 1)

            def take_logits(j, s1_at):
                dve.wait_ge(s1_full, s1_at + 1)
                nc.vector.tensor_copy(logit[:, bass.ds(j, 1), :].rearrange("p o e -> p (o e)"),
                                      S1[:, 0:COLS]).then_inc(s1_used, 1)

            def route_in(s1_at):
                dve.wait_ge(s1_used, s1_at)
                linked(nc.vector.tensor_reduce(row_max[:], logit[:, :, 0:E], AX_X, ALU.max))
                nc.vector.tensor_tensor(ex[:, :, 0:E], logit[:, :, 0:E],
                                        row_max[:].rearrange("p (t o) -> p t o", o=1).to_broadcast([P, TILES, E]),
                                        ALU.subtract).then_inc(ex_in, 1)
                nc.vector.tensor_scalar(ex[:, :, E:COLS], logit[:, :, E:COLS], -1.0, None, ALU.mult).then_inc(ex_in, 1)

            def route_out():
                dve.wait_ge(ex_done, rc.up())
                linked(nc.vector.tensor_scalar(ex[:, :, E:COLS], ex[:, :, E:COLS], 1.0, None, ALU.add))
                nc.vector.reciprocal(comb[:, :, E:COLS], ex[:, :, E:COLS]).then_inc(dve_link, 1)
                link.up()
                for j in range(TILES):
                    nc.vector.max(top[:, j, :], ex[:, j, 0:E]).then_inc(dve_link, 1)
                    link.up()
                dve.wait_ge(dve_link, link.at())
                nc.vector.tensor_reduce(tot[:], top[:], AX_X, ALU.add).then_inc(dve_link, 1)
                link.up()
                for j in range(TILES):
                    nc.vector.match_replace(rest[:, j, :], top[:, j, :], ex[:, j, 0:E], 0.0).then_inc(dve_link, 1)
                    link.up()
                dve.wait_ge(dve_link, link.at())
                linked(nc.vector.reciprocal(rtot[:], tot[:]))
                linked(nc.vector.tensor_tensor(comb[:, :, 0:E], ex[:, :, 0:E], rest[:], ALU.subtract))
                nc.vector.tensor_tensor(comb[:, :, 0:E], comb[:, :, 0:E],
                                        rtot[:].rearrange("p (t o) -> p t o", o=1).to_broadcast([P, TILES, E]),
                                        ALU.mult).then_inc(comb_done, 1)

            def take_comb(s_at, s1_at, k_out):
                if k_out is not None:
                    dve.wait_ge(comb_out, GOLD * k_out)
                for h, (full, used, S, at) in enumerate(((s0_full, s0_used, S0, s_at), (s1_full, s1_used, S1, s1_at))):
                    dve.wait_ge(full, at + 1)
                    nc.vector.tensor_copy(comb_t[:, h * CH:(h + 1) * CH], S[0:COLS, :]).then_inc(used, 1)

            def unit(s, p, c):
                u = s * UNITS + 2 * p + c
                h = hid[:, c, :]
                dve.wait_ge(up_done, u + 1)
                dve.wait_ge(silu_done, u + 1)
                nc.vector.tensor_tensor(h, h, U[:], ALU.mult).then_inc(gated, 1)
                dve.wait_ge(gated, u + 1)
                if c == 0:
                    dve.wait_ge(weight_in[p], 2 * GOLD * (s + 1))
                nc.vector.tensor_tensor(h, h, weight_b[:, p, c * CH:(c + 1) * CH], ALU.mult).then_inc(weighted, 1)
                dve.wait_ge(weighted, u + 1 + WEIGHTED_CREDIT)
                dve.wait_ge(down_done, u + 3)
                nc.vector.tensor_copy(hi_h[:, c, :], h).then_inc(hid_hi, 1)
                dve.wait_ge(hid_hi, u + 1)
                nc.vector.tensor_tensor(lo_h[:, c, :], h, hi_h[:, c, :].bitcast(F32), ALU.subtract).then_inc(hidden, 1)

            def out_copy(k_block, c, s1_before):
                dve.wait_ge(down_done, DOWN_CREDIT + 2 * PAIRS * (k_block + 1) - (1 - c))
                dve.wait_ge(s1_full, s1_before)
                nc.vector.tensor_scalar(ffn_o[:, 1, c * CH:(c + 1) * CH], O[1][c][:], 0.5, None, ALU.mult).then_inc(out1_done, 1)

            def add_out(b, c, at0, at1):
                for g, (full, used, S, at) in enumerate(((s0_full, s0_used, S0, at0), (s1_full, s1_used, S1, at1))):
                    xt = X[:, bass.ds(b * TILES + c * 4 + g * 2, 2), :]
                    dve.wait_ge(full, at + 1)
                    nc.vector.tensor_tensor(xt, xt, S[:].rearrange("p (t c) -> p t c", t=2), ALU.add).then_inc(used, 1)

            def block(ps, b, last):
                k = ps * B + b
                s = k * STEPS
                at0 = S0_AT[ps] + PREP + b * (PREP + 2)
                at1 = S1_AT[ps] + PREP + b * (PREP + 2)
                if not last:
                    with counted_loop(dve, TILES, [link, vc, zc], [2, 1, 1]) as j:
                        t = (b + 1) * TILES + j
                        stats(t, j)
                        vc.up()
                        for p in range(SLOTS):
                            for c in range(CHUNKS):
                                unit(s + j, p, c)
                                if (p, c) == (0, 0):
                                    normalise(t, j, at0 + j)
                                if (p, c) == (1, 1):
                                    low_z((b + 1) % 2, j, at0 + j, at1 + j)
                        take_logits(j, at1 + j)
                    at0, at1 = at0 + TILES, at1 + TILES
                    route_in(at1)
                    for p in range(SLOTS):
                        for c in range(CHUNKS):
                            unit(s + ROUTE, p, c)
                        if p == 1:
                            route_out()
                    take_comb(at0, at1, k + 1)
                    at0, at1 = at0 + 1, at1 + 1
                    for j in range(ROUTE + 1, SEAM):
                        for p in range(SLOTS):
                            for c in range(CHUNKS):
                                unit(s + j, p, c)
                else:
                    with dve.Fori(0, SEAM) as j:
                        for p in range(SLOTS):
                            for c in range(CHUNKS):
                                unit(s + j, p, c)
                for p in range(SLOTS):
                    for c in range(CHUNKS):
                        unit(s + SEAM, p, c)
                s1_before = S1_AT[ps] + PREP + b * (PREP + 2)
                for c in range(CHUNKS):
                    out_copy(k, c, s1_before)
                for c in range(CHUNKS):
                    add_out(b, c, at0 + c, at1 + c)
                dve.wait_ge(s0_used, at0 + CHUNKS)
                dve.wait_ge(s1_used, at1 + CHUNKS)

            def prepare(ps):
                with counted_loop(dve, TILES, [link], [2]) as j:
                    stats(j, j)
                vc.up()
                at0, at1 = S0_AT[ps], S1_AT[ps]
                with counted_loop(dve, TILES, [zc], [1]) as j:
                    normalise(j, j, at0 + j)
                    low_z(0, j, at0 + j, at1 + j)
                    take_logits(j, at1 + j)
                route_in(at1 + TILES)
                route_out()
                take_comb(at0 + TILES, at1 + TILES, ps * B if ps else None)

            LINKS = 2 * TILES + 1 + 2 * TILES + 5

            def dve_pass(ps):
                if ps == 0:
                    dve.wait_ge(x_in[0], GOLD)
                prepare(ps)
                if ps == 0:
                    for b in range(1, B):
                        dve.wait_ge(x_in[b], GOLD)
                with counted_loop(dve, B - 1, [link, vc, zc, rc], [LINKS, TILES, TILES, 1]) as b:
                    block(ps, b, False)
                block(ps, B - 1, True)

            nc.vector.memset(ones[:], 1.0).then_inc(mem_set, 1)
            nc.vector.memset(mean_w[:], 1.0 / P).then_inc(mem_set, 1)
            dve.wait_ge(act_link, 1)
            nc.vector.tensor_scalar(par[:, 0, :], par[:, 0, :], 1e-7, None, ALU.max).then_inc(decay_done, 1)
            dve.wait_ge(table_in, KC)
            for m in range(KC):
                linked(nc.vector.tensor_scalar(inv[:, m, :], scale[:, m, :], 1e-10, None, ALU.max))
                nc.vector.reciprocal(inv[:, m, :], inv[:, m, :]).then_inc(table_done, 2)
            dve.wait_ge(a_hi, 1)
            nc.vector.tensor_tensor(lo_a[:].rearrange("p w k n -> p (w k n)"), raw_a,
                                    hi_a[:].rearrange("p w k n -> p (w k n)").bitcast(F32), ALU.subtract).then_inc(a_lo, 1)
            dve.wait_ge(consts_in[5], GOLD)
            dve_pass(0)

            dve.wait_ge(a_lo, 1)
            dve.wait_ge(mem_set, 2)
            A_LINKS = 2 * TILES + 4 + KC + 4 + 2 + 2 + KC
            with counted_loop(dve, B, [link, vc, zc], [A_LINKS, 1, TILES]) as b:
                with counted_loop(dve, TILES, [link], [2]) as j:
                    stats(b * TILES + j, j)
                vc.up()
                with counted_loop(dve, TILES, [zc], [1]) as j:
                    normalise(b * TILES + j, j, S0_ATT + b * TILES + j)
                    low_z(b % 2, j, S0_ATT + b * TILES + j, None)
                for i in range(4):
                    c, m = divmod(i, KC)
                    q = b * 4 + i
                    dst = state[:, m, c * CH:(c + 1) * CH]
                    dve.wait_ge(k_scaled, q + 1)
                    dve.wait_ge(v_full, q + 1)
                    nc.vector.tensor_tensor(dst, k_s[:, i % 2, :], O[1][i % 2][:], ALU.mult).then_inc(kv_done, 1)
                    dve.wait_ge(kv_done, q + 1 + PROJ_CREDIT)
                    start = 0.0 if c == 0 else state[:, m, c * CH - 1:c * CH]
                    linked(nc.vector.tensor_tensor_scan(dst, ones[:].to_broadcast([P, CH]), dst, start, ALU.mult, ALU.add))
                dve.wait_ge(r_scaled, b * 4 + 4)
                for m in range(KC):
                    linked(nc.vector.tensor_tensor(state[:, m, :], state[:, m, :], r_s[:, m, :], ALU.mult))
                for i in range(4):
                    c, m = divmod(i, KC)
                    linked(nc.vector.bn_stats(bn24[:, i, :], state[:, m, c * CH:(c + 1) * CH]))
                nc.vector.tensor_copy(relay[:], bn24[:, 0, 0:1])
                nc.vector.bn_aggr(gstat[:, 0:2], bn24[:].rearrange("p a s -> p (a s)")).then_inc(part_done, 1)
                dve.wait_ge(avg_done, 2 * b + 1)
                linked(nc.vector.tensor_copy(gstat[:, 2:3], S1[:, 0:1]))
                linked(nc.vector.tensor_tensor(gstat[:, 3:4], gstat[:, 0:1], gstat[:, 2:3], ALU.subtract))
                nc.vector.tensor_scalar(gstat[:, 4:5], gstat[:, 3:4], gstat[:, 3:4], gstat[:, 1:2],
                                        ALU.mult, ALU.add).then_inc(spread_done, 1)
                dve.wait_ge(avg_done, 2 * b + 2)
                nc.vector.tensor_scalar(gstat[:, 5:6], S1[:, 0:1], EPS, None, ALU.add).then_inc(group_var, 1)
                dve.wait_ge(group_rstd, b + 1)
                linked(nc.vector.tensor_scalar(aff[:, 0, :], par[:, 1, :], gstat[:, 6:7], None, ALU.mult))
                linked(nc.vector.tensor_scalar(gstat[:, 6:8], aff[:, 0, :], gstat[:, 2:3], None, ALU.mult))
                nc.vector.tensor_tensor(aff[:, 1, :], par[:, 2, :], gstat[:, 6:8], ALU.subtract).then_inc(affine, 1)
                for m in range(KC):
                    dve.wait_ge(normed, 2 * b + m + 1)
                    if m == 0:
                        dve.wait_ge(wo_done, 4 * b + ONE)
                    linked(nc.vector.tensor_copy(hi_n[:, m, :], state[:, m, :]))
                    nc.vector.tensor_tensor(lo_n[:, m, :], state[:, m, :], hi_n[:, m, :].bitcast(F32),
                                            ALU.subtract).then_inc(n_split, 1)
                for g in range(4):
                    dve.wait_ge(wo_done, 4 * b + g + 1 + ONE)
                    xt = X[:, bass.ds(b * TILES + 2 * g, 2), :]
                    nc.vector.tensor_tensor(xt, xt, O[g // 2][g % 2][:].rearrange("p (t c) -> p t c", t=2),
                                            ALU.add).then_inc(added, 1)
                dve.wait_ge(added, 4 * b + 4 + ONE)
            dve_pass(1)

        @block_ctx.tensor
        def _(pe):
            hl_w, hl_z, hl_h = (hi_w, lo_w), (hi_z, lo_z), (hi_h, lo_h)
            zc = Count()
            cc = Count()

            def project(dst, col, p, zp, c):
                n = 0
                for kc in range(KC):
                    for a, b_ in FIRST_PRODUCTS:
                        mm = nc.tensor.matmul(dst[:], hl_w[a][:, p, col + kc * P:col + (kc + 1) * P],
                                              hl_z[b_][:, zp, kc, c * CH:(c + 1) * CH], start=(n == 0), stop=(n == 5))
                        n += 1
                return mm

            def gate_up(s, p, c, zp):
                u = s * UNITS + 2 * p + c
                if c == 0:
                    pe.wait_ge(w_split, s * SLOTS + p + 1 + SPLIT_CREDIT)
                pe.wait_ge(silu_done, u)
                project(G, 0, p, zp, c).then_inc(gate_done, 1)
                pe.wait_ge(gated, u)
                project(U, KC * P, p, zp, c).then_inc(up_done, 1)

            def down(s, p, c, first=None, last=False):
                u = s * UNITS + 2 * p + c
                pe.wait_ge(hidden, u + 1 + HIDDEN_CREDIT)
                if first is not None:
                    pe.wait_ge(out0_done, first + ONE)
                    pe.wait_ge(out1_done, first + ONE)
                for m in range(KC):
                    for i, (a, b_) in enumerate(FIRST_PRODUCTS):
                        mm = nc.tensor.matmul(O[m][c][:], hl_w[a][:, p, 4 * P + m * P:4 * P + (m + 1) * P],
                                              hl_h[b_][:, c, :], start=(first is not None and i == 0),
                                              stop=(last and i == 2))
                mm.then_inc(down_done, 1)

            def transpose_z(s0_at):
                pe.wait_ge(z_done, zc.up())
                pe.wait_ge(s0_used, s0_at)
                for kc in range(KC):
                    mm = nc.tensor.transpose(S0[:, kc * P:(kc + 1) * P], z[:, kc * P:(kc + 1) * P], ident[:])
                mm.then_inc(s0_full, 1)

            def route_logits(s0_at, s1_at):
                pe.wait_ge(s0_used, s0_at + 1)
                pe.wait_ge(s1_used, s1_at)
                for kc in range(KC):
                    mm = nc.tensor.matmul(S1[:, 0:COLS], zt[:, kc, :], router[:, kc, :], start=(kc == 0), stop=(kc == 1))
                mm.then_inc(s1_full, 1)

            def transpose_comb(s0_at, s1_at):
                pe.wait_ge(comb_done, cc.up())
                for full, used, S, at, h in ((s0_full, s0_used, S0, s0_at, 0), (s1_full, s1_used, S1, s1_at, 1)):
                    pe.wait_ge(used, at)
                    for t in range(4):
                        mm = nc.tensor.transpose(S[0:COLS, t * P:(t + 1) * P], comb[:, h * 4 + t, :], ident[:])
                    mm.then_inc(full, 1)

            def transpose_out(k, c, s0_at, s1_at):
                pe.wait_ge(out0_done, 2 * k + c + 1 + ONE)
                pe.wait_ge(out1_done, 2 * k + c + 1 + ONE)
                for full, used, S, at, g in ((s0_full, s0_used, S0, s0_at, 0), (s1_full, s1_used, S1, s1_at, 1)):
                    pe.wait_ge(used, at)
                    for t in range(2):
                        tok = c * CH + (g * 2 + t) * P
                        for m in range(KC):
                            mm = nc.tensor.transpose(S[:, t * D + m * P:t * D + (m + 1) * P],
                                                     ffn_o[:, m, tok:tok + P], ident[:])
                    mm.then_inc(full, 1)

            def step(s, zp, first=None, seam=False, next_zp=None, side=None):
                for p in range(SLOTS):
                    at_seam = seam and p == SLOTS - 1
                    nxt = (s + (p + 1) // SLOTS, (p + 1) % SLOTS)
                    gate_up(s, p, 1, zp)
                    if side and p == 1:
                        side[0]()
                    fresh = first if p == 0 else None
                    down(s, p, 0, fresh, at_seam)
                    if side and p == 2 and len(side) > 1:
                        side[1]()
                    if not at_seam:
                        gate_up(*nxt, 0, zp)
                    elif next_zp is not None:
                        gate_up(*nxt, 0, next_zp)
                    down(s, p, 1, fresh, at_seam)

            def block(ps, b, last):
                k = ps * B + b
                s, zp = k * STEPS, k % 2
                at0 = S0_AT[ps] + PREP + b * (PREP + 2)
                at1 = S1_AT[ps] + PREP + b * (PREP + 2)
                if not last:
                    step(s, zp, first=2 * k, side=(lambda: transpose_z(at0), lambda: route_logits(at0, at1)))
                    with counted_loop(pe, TILES - 1, [zc], [1]) as i:
                        j = i + 1
                        step(s + j, zp, side=(lambda: transpose_z(at0 + j), lambda: route_logits(at0 + j, at1 + j)))
                    at0, at1 = at0 + TILES, at1 + TILES
                    step(s + ROUTE, zp)
                    transpose_comb(at0, at1)
                    at0, at1 = at0 + 1, at1 + 1
                    for j in range(ROUTE + 1, SEAM):
                        step(s + j, zp)
                else:
                    step(s, zp, first=2 * k)
                    with pe.Fori(1, SEAM) as j:
                        step(s + j, zp)
                step(s + SEAM, zp, seam=True, next_zp=None if last else (k + 1) % 2)
                for c in range(CHUNKS):
                    transpose_out(k, c, at0 + c, at1 + c)

            def pe_pass(ps):
                at0, at1 = S0_AT[ps], S1_AT[ps]
                with counted_loop(pe, TILES, [zc], [1]) as j:
                    transpose_z(at0 + j)
                    route_logits(at0 + j, at1 + j)
                transpose_comb(at0 + TILES, at1 + TILES)
                gate_up(ps * B * STEPS, 0, 0, 0)
                with counted_loop(pe, B - 1, [zc, cc], [TILES, 1]) as b:
                    block(ps, b, False)
                block(ps, B - 1, True)

            pe.wait_ge(consts_in[0], GOLD)
            pe.wait_ge(consts_in[1], GOLD)
            pe_pass(0)

            hl_a, hl_n = (hi_a, lo_a), (hi_n, lo_n)
            pe.wait_ge(a_lo, 1)
            pe.wait_ge(mem_set, 2)
            pe.wait_ge(out0_done, 2 * B + ONE)
            pe.wait_ge(out1_done, 2 * B + ONE)
            pe.wait_ge(silu_done, 2 * PAIRS * B)
            pe.wait_ge(gated, 2 * PAIRS * B)
            with counted_loop(pe, B, [zc], [TILES]) as b:
                with counted_loop(pe, TILES, [zc], [1]) as j:
                    transpose_z(S0_ATT + b * TILES + j)
                pe.wait_ge(s0_used, S0_ATT + (b + 1) * TILES)
                pe.wait_ge(added, 4 * b + ONE)
                for i in range(4):
                    c, m = divmod(i, KC)
                    q = b * 4 + i
                    for w, dst, full, guard in ((1, O[0][i % 2], k_full, k_copied), (2, O[1][i % 2], v_full, kv_done),
                                                (0, G if i % 2 == 0 else U, r_full, r_copied)):
                        if i >= 2:
                            pe.wait_ge(guard, q - 1 + (PROJ_CREDIT if guard is kv_done else 0))
                        n = 0
                        for kc in range(KC):
                            for a, b_ in FIRST_PRODUCTS:
                                mm = nc.tensor.matmul(dst[:], hl_a[a][:, w, kc, m * P:(m + 1) * P],
                                                      hl_z[b_][:, b % 2, kc, c * CH:(c + 1) * CH], start=(n == 0), stop=(n == 5))
                                n += 1
                        mm.then_inc(full, 1)
                pe.wait_ge(part_done, b + 1 + ONE)
                nc.tensor.matmul(S1[:, 0:1], mean_w[:], gstat[:, 0:1], start=True, stop=True).then_inc(avg_done, 1)
                pe.wait_ge(spread_done, b + 1)
                nc.tensor.matmul(S1[:, 0:1], mean_w[:], gstat[:, 4:5], start=True, stop=True).then_inc(avg_done, 1)
                pe.wait_ge(n_split, 2 * b + 2)
                for g in range(4):
                    for t in range(2):
                        tok = (2 * g + t) * P
                        n = 0
                        for kc in range(KC):
                            for a, b_ in FIRST_PRODUCTS:
                                mm = nc.tensor.matmul(O[g // 2][g % 2][:, t * D:(t + 1) * D], hl_n[a][:, kc, tok:tok + P],
                                                      hl_a[b_][:, 3, kc, :], start=(n == 0), stop=(n == 5))
                                n += 1
                    mm.then_inc(wo_done, 1)
            pe_pass(1)


_INS = ["x", "w_pairs", "w_router", "w_attn", "decay", "gn", "eye", "pos"]
_OUT = ((4, 1024, 256), "float32")


def kernel(**inputs):
    import numpy as np
    import concourse.bacc as _bacc
    from concourse import mybir as _mybir
    from concourse.bass_utils import run_bass_kernel_spmd as _run

    a = {k: np.asarray(v) for k, v in inputs.items()}

    def f(name):
        return a["L0_ffn_" + name]

    gu = np.zeros((PAIRS * 2, 2, I, D), np.float32)
    gu[:E] = f("gate_up_proj").reshape(E, 2, I, D)
    gu[E, 0], gu[E, 1] = f("shared_gate_w"), f("shared_up_w")
    dn = np.zeros((PAIRS * 2, D, I), np.float32)
    dn[:E] = f("down_proj")
    dn[E] = f("shared_down_w")
    gu = gu.reshape(PAIRS, 2, 2, I, KC, P).transpose(0, 5, 2, 4, 1, 3).reshape(PAIRS, P, 4 * P)
    dn = dn.reshape(PAIRS, 2, D, I).transpose(0, 1, 3, 2).reshape(PAIRS, P, D)
    att = np.stack([a["L0_attn_" + n].T.reshape(KC, P, D) for n in ("Wr", "Wk", "Wv", "Wo")])
    arrays = {
        "x": a["L0_attn_x"],
        "w_pairs": np.concatenate([gu, dn], axis=2),
        "w_router": np.concatenate([f("router_w"), f("shared_expert_gate_w")]).T.reshape(KC, P, COLS).transpose(1, 0, 2),
        "w_attn": att.transpose(2, 0, 1, 3).reshape(P, 4 * KC * D),
        "decay": a["L0_attn_decay"].reshape(KC, P).T,
        "gn": np.stack([a["L0_attn_gn_weight"], a["L0_attn_gn_bias"]]).reshape(2, KC, P).transpose(2, 0, 1),
        "eye": np.eye(P, dtype=np.float32),
        "pos": np.arange(T, dtype=np.float32).reshape(1, T),
    }
    arrays = {f"in_{k}_dram": np.ascontiguousarray(arrays[k]) for k in _INS}
    nc = _bacc.Bacc("TRN2", target_bir_lowering=False, num_devices=1)
    args = [nc.dram_tensor(k, v.shape, _mybir.dt.from_np(v.dtype), kind="ExternalInput").ap() for k, v in arrays.items()]
    args.append(nc.dram_tensor("out_0_dram", _OUT[0], _mybir.dt.from_np(np.dtype(_OUT[1])), kind="ExternalOutput").ap())
    build(nc, *args)
    r = _run(nc, [arrays], core_ids=[0])
    return r.results[0]["out_0_dram"]
```

```python
from contextlib import ExitStack, contextmanager

import concourse.bass as bass
from concourse import mybir

F32 = mybir.dt.float32
F32R = mybir.dt.float32r
ALU = mybir.AluOpType
ACT = mybir.ActivationFunctionType
AX_X = mybir.AxisListType.X

P = 128
D = 256
KC = D // P
B, T = 4, 1024
TILES = T // P
CH = 512
CHUNKS = T // CH
E, I, TOPK = 64, 64, 8
COLS = E + 1
PAIRS = E // 2 + 1
SLOTS = 3
STEPS = PAIRS // SLOTS
PAIR_W = 4 * P + D
QUAD = TILES // CHUNKS
TAIL = STEPS - TILES
BLOCKS = 2 * B
EPS = 1e-5
GOLD = 16
FIRST_PRODUCTS = ((0, 0), (0, 1), (1, 0))
assert PAIRS == STEPS * SLOTS and TAIL == SLOTS

SPLIT_CREDIT = SLOTS
DOWN_CREDIT = 4
WEIGHTED_CREDIT = 2 * SLOTS
HIDDEN_CREDIT = 2
ONE = 1


class Count:

    def __init__(self, start=0):
        self.base, self.off = start, 0

    def at(self, more=0):
        return self.base + (self.off + more) if self.off + more else self.base

    def up(self):
        self.off += 1
        return self.at()


@contextmanager
def counted_loop(eng, times, counts, per):
    before = [(c.base, c.off) for c in counts]
    with eng.Fori(0, times) as i:
        for c, (base, off), k in zip(counts, before, per):
            c.base, c.off = base + i * k + off, 0
        yield i
        for c, k in zip(counts, per):
            assert c.off == k, (c.off, k)
    for c, (base, off), k in zip(counts, before, per):
        c.base, c.off = base, off + times * k


def build(nc, x, w_pairs, w_router, w_attn, decay, gn, eye, pos, out):
    with ExitStack() as ctx:
        def sb(name, shape, dt=F32):
            return ctx.enter_context(nc.sbuf_tensor(name, shape, dt))

        def bank(name):
            return ctx.enter_context(nc.psum_tensor(name, [P, CH], F32))

        def sem(name):
            return ctx.enter_context(nc.semaphore(name))

        X = sb("X", [P, B * TILES, D])
        raw_w = sb("raw_w", [P, SLOTS, PAIR_W])
        hi_w = sb("hi_w", [P, SLOTS, PAIR_W], F32R)
        lo_w = sb("lo_w", [P, SLOTS, PAIR_W], F32R)
        hi_z = sb("hi_z", [P, 2, KC, T], F32R)
        lo_z = sb("lo_z", [P, 2, KC, T], F32R)
        weight_b = sb("weight_b", [P, SLOTS, T])
        hid = sb("hid", [P, 2, CH])
        hi_h = sb("hi_h", [P, 2, CH], F32R)
        lo_h = sb("lo_h", [P, 2, CH], F32R)
        zero_f = sb("zero_f", [P, P])
        zero_w = sb("zero_w", [P, P], F32R)
        ffn_o = sb("ffn_o", [P, KC, T])
        z = sb("z", [P, D])
        zt = sb("zt", [P, KC, P])
        bn6 = sb("bn6", [P, 6])
        relay = sb("relay", [P, 1])
        mv = sb("mv", [P, 2])
        mean = sb("mean", [P, TILES])
        ve = sb("ve", [P, TILES])
        rstd = sb("rstd", [P, TILES])
        mhalf = sb("mhalf", [P, TILES])
        logit = sb("logit", [P, TILES, COLS])
        row_max = sb("row_max", [P, TILES])
        ex = sb("ex", [P, TILES, COLS])
        top = sb("top", [P, TILES, TOPK])
        rest = sb("rest", [P, TILES, E])
        tot = sb("tot", [P, TILES])
        rtot = sb("rtot", [P, TILES])
        comb = sb("comb", [P, TILES, COLS])
        comb_t = sb("comb_t", [COLS, T])
        ident = sb("ident", [P, P])
        router = sb("router", [P, KC, COLS])
        hi_a = sb("hi_a", [P, 4, KC, D], F32R)
        lo_a = sb("lo_a", [P, 4, KC, D], F32R)
        z_a = sb("z_a", [P, D])
        hi_za = sb("hi_za", [P, KC, CH], F32R)
        lo_za = sb("lo_za", [P, KC, CH], F32R)
        mean_a = sb("mean_a", [P, QUAD])
        ve_a = sb("ve_a", [P, QUAD])
        rstd_a = sb("rstd_a", [P, QUAD])
        r_s = sb("r_s", [P, CH])
        k_s = sb("k_s", [P, CH])
        carry = sb("carry", [P, KC])
        state = sb("state", [P, KC, T])
        half_scale = sb("half_scale", [P, KC, T])
        inv = sb("inv", [P, KC, T])
        hi_n = sb("hi_n", [P, KC, CH], F32R)
        lo_n = sb("lo_n", [P, KC, CH], F32R)
        ones = sb("ones", [P, 1])
        mean_w = sb("mean_w", [P, P])
        par = sb("par", [P, 3, KC])
        bn24 = sb("bn24", [P, 4, 6])
        gstat = sb("gstat", [P, 8])
        aff = sb("aff", [P, 2, KC])

        O = [[bank(f"O{m}{c}") for c in range(CHUNKS)] for m in range(KC)]
        G, U, S0, S1 = bank("G"), bank("U"), bank("S0"), bank("S1")
        comb_d = nc.dram_tensor("comb_scratch", (2, COLS, T), F32).ap()
        raw_a = state[:, :, :].rearrange("p k t -> p (k t)")
        pos_b = ffn_o[:, 0, :]

        x_in = [sem(f"x_in{b}") for b in range(B)]
        consts_in = [sem(f"consts_in{i}") for i in range(7)]
        w_in = [sem(f"w_in{i}") for i in range(SLOTS)]
        weight_in = [sem(f"weight_in{i}") for i in range(SLOTS)]
        w_hi, w_split = sem("w_hi"), sem("w_split")
        gate_done, up_done, down_done = sem("gate_done"), sem("up_done"), sem("down_done")
        silu_done, gated, weighted, hid_hi, hidden = (sem(n) for n in ("silu_done", "gated", "weighted", "hid_hi", "hidden"))
        out0_done, out1_done = sem("out0_done"), sem("out1_done")
        s0_full, s0_used, s1_full, s1_used = (sem(n) for n in ("s0_full", "s0_used", "s1_full", "s1_used"))
        mean_done = sem("mean_done")
        var_done, rstd_done, z_done, z_hi = sem("var_done"), sem("rstd_done"), sem("z_done"), sem("z_hi")
        ex_in, ex_done, comb_done, comb_out = (sem(n) for n in ("ex_in", "ex_done", "comb_done", "comb_out"))
        dve_link, act_link = sem("dve_link"), sem("act_link")
        mem_set, exponent_set = sem("mem_set"), sem("exponent_set")
        var_a_done, rstd_a_done, za_done, za_hi = sem("var_a_done"), sem("rstd_a_done"), sem("za_done"), sem("za_hi")
        k_scaled = sem("k_scaled")
        part_done, spread_done, group_rstd, affine, normed, n_split = (
            sem(n) for n in ("part_done", "spread_done", "group_rstd", "affine", "normed", "n_split"))
        a_hi, a_lo, table_done, table_in, decay_done = sem("a_hi"), sem("a_lo"), sem("table_done"), sem("table_in"), sem("decay_done")
        stored = sem("stored")

        F_AT = {False: (0, 1, 2, 3), True: (0, 2, 5, 7)}
        L_AT = {False: (0, 1, 2, 3), True: (0, 3, 6, 9)}
        A_AT = ((0, 1), (1, 1), (1, 2), (0, 3))
        K_AT, V_AT, R_AT = (4, 6), (4, 7), (5, 8)
        QUAD_USES = {False: (4, 4), True: (8, 10)}
        COMB_AT = {False: (0, 0), True: (0, 2)}
        MEAN_AT, VAR_AT = 0, 1
        WO_AT = (1, 3)
        OUT_AT = {False: (1, 1), True: (3, 5)}
        USES = {a: tuple(CHUNKS * QUAD_USES[a][i] + OUT_AT[a][i] + CHUNKS for i in range(2)) for a in (False, True)}
        UNITS = 2 * SLOTS
        FIRST = (ONE + TILES + 1, ONE + TILES + 1)

        def walk(eng, block, counts=(), quiet=(), busy=()):
            at = FIRST
            block(0, 0, at, True, False)
            at = tuple(x + y for x, y in zip(at, USES[False]))
            with counted_loop(eng, B, list(counts), list(busy)) as b:
                block(b + 1, (b + 1) % B, tuple(x + b * y for x, y in zip(at, USES[True])), True, True)
            at = tuple(x + B * y for x, y in zip(at, USES[True]))
            with counted_loop(eng, 2, list(counts), list(quiet)) as b:
                block(b + B + 1, b + 1, tuple(x + b * y for x, y in zip(at, USES[False])), True, False)
            at = tuple(x + 2 * y for x, y in zip(at, USES[False]))
            block(BLOCKS - 1, B - 1, at, False, False)

        blk = nc.Block()
        block_ctx = ctx.enter_context(blk)

        @block_ctx.sync
        def _(sp):
            def load_w(pair, n, p):
                sp.wait_ge(w_split, n + 1)
                sp.dma_start(raw_w[:, p, :], w_pairs[pair]).then_inc(w_in[p], GOLD)

            def step(k, j, seam=False, final=False):
                s = k * STEPS + j
                for p in range(SLOTS):
                    n = s * SLOTS + p
                    if not (seam and p > 0):
                        load_w(j * SLOTS + p + 2, n + 2, (p + 2) % SLOTS)
                    elif not final:
                        load_w(p - 1, n + 2, p - 1)
                    if p == 0 and isinstance(j, int) and j == 0:
                        sp.wait_ge(comb_out, GOLD * (k + 1))
                    sp.wait_ge(weighted, 2 * n + 2)
                    for half in range(2):
                        e = E if (seam and p == SLOTS - 1) else (j * SLOTS + p) * 2 + half
                        sp.dma_start(weight_b[half * I:(half + 1) * I, p, :],
                                     comb_d[bass.ds(k % 2, 1), bass.ds(e, 1), :]
                                     .rearrange("o e t -> (o e) t").to_broadcast([I, T])).then_inc(weight_in[p], GOLD)

            def block(k, fb, at, prep, attn):
                step(k, 0)
                with sp.Fori(1, STEPS - 1) as j:
                    step(k, j)
                step(k, STEPS - 1, True, not prep)

            sp.dma_start(par[:, 0, :], decay).then_inc(consts_in[4], GOLD)
            sp.dma_start(pos_b, pos.to_broadcast([P, T])).then_inc(consts_in[3], GOLD)
            sp.dma_start(X[:, 0:TILES, :], x[0].rearrange("(t p) c -> p t c", p=P)).then_inc(x_in[0], GOLD)
            sp.dma_start(ident[:], eye).then_inc(consts_in[0], GOLD)
            sp.dma_start(router[:], w_router).then_inc(consts_in[1], GOLD)
            load_w(0, 0, 0)
            load_w(1, 1, 1)
            sp.dma_start(raw_a, w_attn).then_inc(consts_in[2], GOLD)
            sp.dma_start(par[:, 1:3, :], gn).then_inc(consts_in[5], GOLD)
            for b in range(1, B):
                sp.dma_start(X[:, b * TILES:(b + 1) * TILES, :],
                             x[b].rearrange("(t p) c -> p t c", p=P)).then_inc(x_in[b], GOLD)
            walk(sp, block)

        @block_ctx.gpsimd
        def _(pool):
            pool.sem_inc(w_split, SPLIT_CREDIT)
            pool.sem_inc(down_done, DOWN_CREDIT)
            pool.sem_inc(weighted, WEIGHTED_CREDIT)
            pool.sem_inc(hidden, HIDDEN_CREDIT)
            for guard in (s0_full, s0_used, s1_full, s1_used, out0_done, out1_done, za_done):
                pool.sem_inc(guard, ONE)
            pool.memset(mhalf[:], -0.5).then_inc(exponent_set, 1)
            pool.wait_ge(exponent_set, 1)

            def split_lo(s, p):
                n = s * SLOTS + p
                pool.wait_ge(w_hi, n + 1)
                pool.tensor_tensor(lo_w[:, p, :], raw_w[:, p, :], hi_w[:, p, :].bitcast(F32),
                                   ALU.subtract).then_inc(w_split, 1)

            def rstd_of(j, n, tiles):
                pool.wait_ge(var_done, tiles)
                pool.tensor_tensor(rstd[:, bass.ds(j, n)], ve[:, bass.ds(j, n)], mhalf[:, 0:n], ALU.pow).then_inc(rstd_done, 1)

            def attend(k, at, c, q):
                batch = k - 1
                if q < QUAD:
                    pool.wait_ge(var_a_done, batch * TILES + c * QUAD + q + 1)
                    pool.tensor_tensor(rstd_a[:, q:q + 1], ve_a[:, q:q + 1], mhalf[:, 0:1], ALU.pow).then_inc(rstd_a_done, 1)
                if q in (6, 8):
                    m = (6, 8).index(q)
                    pool.wait_ge(s0_used, at[0] + K_AT[m] + 1)
                    pool.wait_ge(table_done, KC)
                    pool.tensor_tensor(k_s[:], k_s[:], inv[:, m, bass.ds(c * CH, CH)], ALU.mult).then_inc(k_scaled, 1)

            def block(k, fb, at, prep, attn):
                s = k * STEPS
                if prep:
                    with pool.Fori(0, CHUNKS) as c:
                        for i in range(QUAD):
                            for p in range(SLOTS):
                                q = i * SLOTS + p
                                split_lo(s + c * QUAD + i + (p + 2) // SLOTS, (p + 2) % SLOTS)
                                if p == 0:
                                    rstd_of(c * QUAD + i, 1, (k + 1) * TILES + c * QUAD + i + 1)
                                if attn:
                                    attend(k, [a + c * u for a, u in zip(at, QUAD_USES[True])], c, q)
                else:
                    with pool.Fori(0, TILES) as j:
                        for p in range(SLOTS):
                            split_lo(s + j + (p + 2) // SLOTS, (p + 2) % SLOTS)
                if not attn and not isinstance(k, int) or not prep:
                    store(fb - 1, at)
                for i in range(TAIL):
                    for p in range(SLOTS):
                        if prep or (i, p) < (TAIL - 1, 1):
                            split_lo(s + TILES + i + (p + 2) // SLOTS, (p + 2) % SLOTS)
                        if attn and (i, p) == (0, 2):
                            pool.wait_ge(s1_used, at[1] + CHUNKS * QUAD_USES[True][1] + VAR_AT + 1)
                            pool.tensor_tensor(gstat[:, 6:7], gstat[:, 5:6], mhalf[:, 0:1], ALU.pow).then_inc(group_rstd, 1)

            def store(b, at):
                pool.wait_ge(s0_used, at[0])
                pool.wait_ge(s1_used, at[1])
                pool.dma_start(out[bass.ds(b, 1), :, :].rearrange("o (t p) c -> p (o t) c", p=P),
                               X[:, bass.ds(b * TILES, TILES), :]).then_inc(stored, GOLD)

            split_lo(0, 0)
            split_lo(0, 1)
            rstd_of(0, TILES, TILES)
            walk(pool, block)
            end = tuple(f + 4 * a + 3 * n + 2 for f, a, n in zip(FIRST, USES[True], USES[False]))
            store(B - 1, end)
            pool.wait_ge(stored, B * GOLD)

        @block_ctx.scalar
        def _(act):
            def split_hi(s, p):
                n = s * SLOTS + p
                act.wait_ge(w_in[p], GOLD * (s + 1))
                act.wait_ge(down_done, 2 * n)
                nc.scalar.activation(hi_w[:, p, :], raw_w[:, p, :], ACT.Copy).then_inc(w_hi, 1)

            def silu(s, p, c):
                u = s * UNITS + 2 * p + c
                act.wait_ge(gate_done, u + 1)
                act.wait_ge(hidden, u + HIDDEN_CREDIT - 1)
                nc.scalar.activation(hid[:, c, :], G[:], ACT.Silu).then_inc(silu_done, 1)

            def high_z(zp, j, s0_at):
                act.wait_ge(s0_full, s0_at + 1)
                nc.scalar.activation(hi_z[:, zp, :, bass.ds(j * P, P)],
                                     S0[:, 0:D].rearrange("p (k t) -> p k t", k=KC), ACT.Copy).then_inc(z_hi, 1)

            def exps(k):
                act.wait_ge(ex_in, 2 * k + 2)
                nc.scalar.activation(ex[:], ex[:], ACT.Exp).then_inc(ex_done, 1)

            def store_comb(k, s0_at, s1_at):
                act.wait_ge(s0_used, s0_at + 1)
                act.wait_ge(s1_used, s1_at + 1)
                act.dma_start(comb_d[bass.ds(k % 2, 1)].rearrange("o e t -> (o e) t"), comb_t[:]).then_inc(comb_out, GOLD)

            def out_copy(k, c, s1_before):
                act.wait_ge(down_done, DOWN_CREDIT + 2 * PAIRS * (k + 1) - (1 - c))
                act.wait_ge(s1_full, s1_before)
                nc.scalar.activation(ffn_o[:, 0, c * CH:(c + 1) * CH], O[0][c][:], ACT.Copy, scale=0.5).then_inc(out0_done, 1)

            def attend(k, at, c, q):
                batch = k - 1
                if 2 <= q <= 5:
                    j = q - 2
                    which, use = A_AT[j]
                    act.wait_ge((s0_full, s1_full)[which], at[which] + use + 1)
                    nc.scalar.activation(hi_za[:, :, j * P:(j + 1) * P],
                                         (S0, S1)[which][:, 0:D].rearrange("p (k t) -> p k t", k=KC),
                                         ACT.Copy).then_inc(za_hi, 1)
                if q in (6, 8):
                    m = (6, 8).index(q)
                    act.wait_ge(s0_full, at[0] + K_AT[m] + 1)
                    nc.scalar.activation(k_s[:], S0[:], ACT.Copy).then_inc(s0_used, 1)
                if q in (7, 10):
                    m = (7, 10).index(q)
                    act.wait_ge(s1_full, at[1] + R_AT[m] + 1)
                    nc.scalar.activation(r_s[:], S1[:], ACT.Tanh, scale=0.5).then_inc(s1_used, 1)

            def normalise_batch(c):
                for m in range(KC):
                    nc.scalar.activation(state[:, m, c * CH:(c + 1) * CH], state[:, m, c * CH:(c + 1) * CH], ACT.Identity,
                                         bias=aff[:, 1, m:m + 1], scale=aff[:, 0, m:m + 1]).then_inc(normed, 1)

            def pair(s, i, p, mid=None):
                split_hi(s + (p + 2) // SLOTS, (p + 2) % SLOTS)
                nxt = (s + (p + 1) // SLOTS, (p + 1) % SLOTS)
                silu(*nxt, 0)
                if mid:
                    mid()
                silu(*nxt, 1)

            def block(k, fb, at, prep, attn):
                s = k * STEPS
                if prep:
                    with act.Fori(0, CHUNKS) as c:
                        atc = [a + c * u for a, u in zip(at, QUAD_USES[attn])]
                        for i in range(QUAD):
                            for p in range(SLOTS):
                                def mid():
                                    if p == 1:
                                        high_z((k + 1) % 2, c * QUAD + i, atc[0] + F_AT[attn][i])
                                    if attn:
                                        attend(k, atc, c, i * SLOTS + p)
                                pair(s + c * QUAD + i, i, p, mid)
                    tail = [a + CHUNKS * u for a, u in zip(at, QUAD_USES[attn])]
                else:
                    with act.Fori(0, TILES) as j:
                        for p in range(SLOTS):
                            pair(s + j, 0, p)
                s = s + TILES
                for i in range(TAIL):
                    for p in range(SLOTS):
                        if (i, p) == (TAIL - 1, SLOTS - 1):
                            break
                        if not prep and (i, p) == (TAIL - 1, 1):
                            silu(s + i, 2, 0)
                            silu(s + i, 2, 1)
                            break
                        pair(s + i, i, p)
                        if prep and (i, p) == (0, 0):
                            exps(k + 1)
                        if prep and (i, p) == (1, 0):
                            store_comb(k + 1, tail[0] + COMB_AT[attn][0], tail[1] + COMB_AT[attn][1])
                        if attn and (i, p) == (1, 0):
                            act.wait_ge(affine, k)
                            normalise_batch(0)
                        if attn and (i, p) == (1, 1):
                            normalise_batch(1)
                s = s + TAIL - 1
                if prep:
                    split_hi(s + 1, 1)
                out_copy(k, 0, at[1])
                if prep:
                    silu(s + 1, 0, 0)
                out_copy(k, 1, at[1])
                if prep:
                    silu(s + 1, 0, 1)

            act.wait_ge(consts_in[4], GOLD)
            nc.scalar.activation(par[:, 0, :], par[:, 0, :], ACT.Sigmoid).then_inc(act_link, 1)
            act.wait_ge(decay_done, 1)
            nc.scalar.activation(par[:, 0, :], par[:, 0, :], ACT.Ln).then_inc(act_link, 1)
            act.wait_ge(act_link, 2)
            act.wait_ge(consts_in[3], GOLD)
            for m in range(KC):
                nc.scalar.activation(half_scale[:, m, :], pos_b, ACT.Exp, scale=par[:, 0, m:m + 1]).then_inc(table_in, 1)
            split_hi(0, 0)
            split_hi(0, 1)
            with act.Fori(0, TILES) as j:
                high_z(0, j, ONE + j)
            exps(0)
            store_comb(0, ONE + TILES, ONE + TILES)
            act.wait_ge(consts_in[2], GOLD)
            nc.scalar.activation(hi_a[:].rearrange("p w k n -> p (w k n)"), raw_a, ACT.Copy).then_inc(a_hi, 1)
            silu(0, 0, 0)
            silu(0, 0, 1)
            walk(act, block)

        @block_ctx.vector
        def _(dve):
            link = Count()

            def linked(ins):
                ins.then_inc(dve_link, 1)
                dve.wait_ge(dve_link, link.up())

            def stats(t, mean_to, ve_to, done):
                linked(nc.vector.bn_stats(bn6[:], X[:, bass.ds(t, 1), :].rearrange("p o c -> p (o c)")))
                nc.vector.tensor_copy(relay[:], bn6[:, 0:1])
                linked(nc.vector.bn_aggr(mv[:], bn6[:]))
                nc.vector.tensor_copy(mean_to, mv[:, 0:1]).then_inc(mean_done, 1)
                nc.vector.tensor_scalar(ve_to, mv[:, 1:2], EPS, None, ALU.add).then_inc(done, 1)

            def ffn_stats(t, j):
                stats(t, mean[:, bass.ds(j, 1)], ve[:, bass.ds(j, 1)], var_done)

            def normalise(t, j, rounds, s0_before):
                dve.wait_ge(rstd_done, rounds)
                dve.wait_ge(s0_full, s0_before)
                nc.vector.tensor_scalar(z[:], X[:, bass.ds(t, 1), :].rearrange("p o c -> p (o c)"), mean[:, bass.ds(j, 1)],
                                        rstd[:, bass.ds(j, 1)], ALU.subtract, ALU.mult).then_inc(z_done, 1)

            def low_z(zp, j, tile, s1_before):
                dve.wait_ge(z_hi, tile + 1)
                src = S0[:, 0:D].rearrange("p (k t) -> p k t", k=KC)
                nc.vector.tensor_tensor(lo_z[:, zp, :, bass.ds(j * P, P)], src,
                                        hi_z[:, zp, :, bass.ds(j * P, P)].bitcast(F32), ALU.subtract)
                dve.wait_ge(s1_full, s1_before)
                nc.vector.tensor_copy(zt[:], src).then_inc(s0_used, 1)

            def take_logits(j, s1_at):
                dve.wait_ge(s1_full, s1_at + 1)
                nc.vector.tensor_copy(logit[:, bass.ds(j, 1), :].rearrange("p o e -> p (o e)"),
                                      S1[:, 0:COLS]).then_inc(s1_used, 1)

            def route_in(s1_at):
                dve.wait_ge(s1_used, s1_at)
                linked(nc.vector.tensor_reduce(row_max[:], logit[:, :, 0:E], AX_X, ALU.max))
                nc.vector.tensor_tensor(ex[:, :, 0:E], logit[:, :, 0:E],
                                        row_max[:].rearrange("p (t o) -> p t o", o=1).to_broadcast([P, TILES, E]),
                                        ALU.subtract).then_inc(ex_in, 1)
                nc.vector.tensor_scalar(ex[:, :, E:COLS], logit[:, :, E:COLS], -1.0, None, ALU.mult).then_inc(ex_in, 1)

            def route_out(k):
                dve.wait_ge(ex_done, k + 1)
                linked(nc.vector.tensor_scalar(ex[:, :, E:COLS], ex[:, :, E:COLS], 1.0, None, ALU.add))
                nc.vector.reciprocal(comb[:, :, E:COLS], ex[:, :, E:COLS]).then_inc(dve_link, 1)
                link.up()
                for j in range(TILES):
                    nc.vector.max(top[:, j, :], ex[:, j, 0:E]).then_inc(dve_link, 1)
                    link.up()
                dve.wait_ge(dve_link, link.at())
                nc.vector.tensor_reduce(tot[:], top[:], AX_X, ALU.add).then_inc(dve_link, 1)
                link.up()
                for j in range(TILES):
                    nc.vector.match_replace(rest[:, j, :], top[:, j, :], ex[:, j, 0:E], 0.0).then_inc(dve_link, 1)
                    link.up()
                dve.wait_ge(dve_link, link.at())
                linked(nc.vector.reciprocal(rtot[:], tot[:]))
                linked(nc.vector.tensor_tensor(comb[:, :, 0:E], ex[:, :, 0:E], rest[:], ALU.subtract))
                nc.vector.tensor_tensor(comb[:, :, 0:E], comb[:, :, 0:E],
                                        rtot[:].rearrange("p (t o) -> p t o", o=1).to_broadcast([P, TILES, E]),
                                        ALU.mult).then_inc(comb_done, 1)

            def take_comb(k, s0_at, s1_at):
                if not isinstance(k, int) or k > 0:
                    dve.wait_ge(comb_out, GOLD * k)
                for h, (full, used, S, at) in enumerate(((s0_full, s0_used, S0, s0_at), (s1_full, s1_used, S1, s1_at))):
                    dve.wait_ge(full, at + 1)
                    nc.vector.tensor_copy(comb_t[:, h * CH:(h + 1) * CH], S[0:COLS, :]).then_inc(used, 1)

            def unit(s, p, c):
                u = s * UNITS + 2 * p + c
                h = hid[:, c, :]
                dve.wait_ge(up_done, u + 1)
                dve.wait_ge(silu_done, u + 1)
                nc.vector.tensor_tensor(h, h, U[:], ALU.mult).then_inc(gated, 1)
                dve.wait_ge(gated, u + 1)
                if c == 0:
                    dve.wait_ge(weight_in[p], 2 * GOLD * (s + 1))
                nc.vector.tensor_tensor(h, h, weight_b[:, p, c * CH:(c + 1) * CH], ALU.mult).then_inc(weighted, 1)
                dve.wait_ge(weighted, u + 1 + WEIGHTED_CREDIT)
                dve.wait_ge(down_done, u + 3)
                nc.vector.tensor_copy(hi_h[:, c, :], h).then_inc(hid_hi, 1)
                dve.wait_ge(hid_hi, u + 1)
                nc.vector.tensor_tensor(lo_h[:, c, :], h, hi_h[:, c, :].bitcast(F32), ALU.subtract).then_inc(hidden, 1)

            def out_copy(k, c, s1_before):
                dve.wait_ge(down_done, DOWN_CREDIT + 2 * PAIRS * (k + 1) - (1 - c))
                dve.wait_ge(s1_full, s1_before)
                nc.vector.tensor_scalar(ffn_o[:, 1, c * CH:(c + 1) * CH], O[1][c][:], 0.5, None, ALU.mult).then_inc(out1_done, 1)

            def add_to_x(b, c, at0, at1):
                for g, (full, used, S, at) in enumerate(((s0_full, s0_used, S0, at0), (s1_full, s1_used, S1, at1))):
                    xt = X[:, bass.ds(b * TILES + c * QUAD + g * 2, 2), :]
                    dve.wait_ge(full, at + 1)
                    nc.vector.tensor_tensor(xt, xt, S[:].rearrange("p (t c) -> p t c", t=2), ALU.add).then_inc(used, 1)

            def attend_x(k, at, c, q):
                batch = k - 1
                st = bass.ds(c * CH, CH)
                if q < QUAD:
                    stats(batch * TILES + c * QUAD + q, mean_a[:, q:q + 1], ve_a[:, q:q + 1], var_a_done)
                if q in (7, 10):
                    m = (7, 10).index(q)
                    dve.wait_ge(s1_used, at[1] + V_AT[m] + 1)
                    linked(nc.vector.tensor_tensor_scan(state[:, m, st], ones[:].to_broadcast([P, CH]), state[:, m, st],
                                                        carry[:, m:m + 1], ALU.mult, ALU.add))
                    linked(nc.vector.tensor_copy(carry[:, m:m + 1], state[:, m, bass.ds(c * CH + CH - 1, 1)]))
                if q in (8, 11):
                    m = (8, 11).index(q)
                    dve.wait_ge(s1_used, at[1] + R_AT[m] + 1)
                    linked(nc.vector.scalar_tensor_tensor(out=state[:, m, st], in0=r_s[:], scalar=1.0, in1=state[:, m, st],
                                                          op0=ALU.add, op1=ALU.mult))
                    linked(nc.vector.tensor_tensor(state[:, m, st], state[:, m, st], half_scale[:, m, st], ALU.mult))
                    linked(nc.vector.bn_stats(bn24[:, bass.ds(c * KC + m, 1), :].rearrange("p o s -> p (o s)"),
                                              state[:, m, st]))

            def attend_y(k, at, c, q):
                batch = k - 1
                tile = batch * TILES + c * QUAD
                if 2 <= q <= 5:
                    j = q - 2
                    which, use = A_AT[j]
                    dve.wait_ge(za_hi, tile + j + 1)
                    nc.vector.tensor_tensor(lo_za[:, :, j * P:(j + 1) * P],
                                            (S0, S1)[which][:, 0:D].rearrange("p (k t) -> p k t", k=KC),
                                            hi_za[:, :, j * P:(j + 1) * P].bitcast(F32),
                                            ALU.subtract).then_inc((s0_used, s1_used)[which], 1)
                if 1 <= q <= 4:
                    j = q - 1
                    dve.wait_ge(rstd_a_done, tile + j + 1)
                    if j:
                        which, use = A_AT[j - 1]
                        dve.wait_ge((s0_full, s1_full)[which], at[which] + use + 1)
                    nc.vector.tensor_scalar(z_a[:], X[:, bass.ds(tile + j, 1), :].rearrange("p o c -> p (o c)"),
                                            mean_a[:, j:j + 1], rstd_a[:, j:j + 1], ALU.subtract, ALU.mult).then_inc(za_done, 1)
                if q in (6, 9):
                    m = (6, 9).index(q)
                    dve.wait_ge(k_scaled, (batch * CHUNKS + c) * KC + m + 1)
                    dve.wait_ge(s1_full, at[1] + V_AT[m] + 1)
                    nc.vector.tensor_tensor(state[:, m, bass.ds(c * CH, CH)], k_s[:], S1[:], ALU.mult).then_inc(s1_used, 1)

            def split_n(c, m, k):
                dve.wait_ge(normed, 4 * (k - 1) + 2 * c + m + 1)
                src = state[:, m, c * CH:(c + 1) * CH]
                linked(nc.vector.tensor_copy(hi_n[:, m, :], src))
                nc.vector.tensor_tensor(lo_n[:, m, :], src, hi_n[:, m, :].bitcast(F32), ALU.subtract).then_inc(n_split, 1)

            def attend_tail(k, at, tail, pos):
                batch = k - 1
                if pos == (0, 1):
                    nc.vector.tensor_copy(relay[:], bn24[:, 0, 0:1])
                    nc.vector.bn_aggr(gstat[:, 0:2], bn24[:].rearrange("p a s -> p (a s)")).then_inc(part_done, 1)
                if pos == (1, 1):
                    dve.wait_ge(s1_full, tail[1] + MEAN_AT + 1)
                    nc.vector.tensor_copy(gstat[:, 2:3], S1[:, 0:1]).then_inc(s1_used, 1)
                    dve.wait_ge(s1_used, tail[1] + MEAN_AT + 1)
                    linked(nc.vector.tensor_tensor(gstat[:, 3:4], gstat[:, 0:1], gstat[:, 2:3], ALU.subtract))
                    nc.vector.tensor_scalar(gstat[:, 4:5], gstat[:, 3:4], gstat[:, 3:4], gstat[:, 1:2],
                                            ALU.mult, ALU.add).then_inc(spread_done, 1)
                if pos == (2, 1):
                    dve.wait_ge(s1_full, tail[1] + VAR_AT + 1)
                    nc.vector.tensor_scalar(gstat[:, 5:6], S1[:, 0:1], EPS, None, ALU.add).then_inc(s1_used, 1)
                if pos == (3, 0):
                    dve.wait_ge(group_rstd, k)
                    linked(nc.vector.tensor_scalar(aff[:, 0, :], par[:, 1, :], gstat[:, 6:7], None, ALU.mult))
                    linked(nc.vector.tensor_scalar(gstat[:, 6:8], aff[:, 0, :], gstat[:, 2:3], None, ALU.mult))
                    nc.vector.tensor_tensor(aff[:, 1, :], par[:, 2, :], gstat[:, 6:8], ALU.subtract).then_inc(affine, 1)
                if pos[0] in (4, 6):
                    split_n((pos[0] - 4) // 2, pos[1], k)
                if pos[0] in (5, 7) and pos[1] == 1:
                    c = (pos[0] - 5) // 2
                    add_to_x(batch, c, tail[0] + WO_AT[0] + c, tail[1] + WO_AT[1] + c)

            def block(k, fb, at, prep, attn):
                s = k * STEPS
                nb = (fb + 1) % B if isinstance(k, int) or attn else fb + 1
                if attn:
                    nc.vector.memset(carry[:], 0.0).then_inc(dve_link, 1)
                    link.up()
                if prep:
                    uses = QUAD_USES[attn]
                    with counted_loop(dve, CHUNKS, [link], [CHUNK_LINKS[attn]]) as c:
                        atc = [a + c * u for a, u in zip(at, uses)]
                        for i in range(QUAD):
                            j = c * QUAD + i
                            tile = (k + 1) * TILES + j
                            for p in range(SLOTS):
                                q = i * SLOTS + p
                                nxt = (s + j + (p + 1) // SLOTS, (p + 1) % SLOTS)
                                unit(*nxt, 0)
                                if p == 0:
                                    ffn_stats(nb * TILES + j, j)
                                if attn:
                                    attend_x(k, atc, c, q)
                                unit(*nxt, 1)
                                if p == 0:
                                    normalise(nb * TILES + j, j, (k * TILES + j) + 2, atc[0] + F_AT[attn][i])
                                if p == 1:
                                    low_z((k + 1) % 2, j, tile, atc[1] + L_AT[attn][i])
                                if p == 2:
                                    take_logits(j, atc[1] + L_AT[attn][i])
                                if attn:
                                    attend_y(k, atc, c, q)
                    tail = [a + CHUNKS * u for a, u in zip(at, uses)]
                    out_at = [a + u for a, u in zip(tail, OUT_AT[attn])]
                else:
                    with dve.Fori(0, TILES) as j:
                        for p in range(SLOTS):
                            for c in range(CHUNKS):
                                unit(s + j + (p + 1) // SLOTS, (p + 1) % SLOTS, c)
                    out_at = at
                s = s + TILES
                for t in range(TAIL * SLOTS - 1):
                    nxt = (s + (t + 1) // SLOTS, (t + 1) % SLOTS)
                    for c in range(CHUNKS):
                        unit(*nxt, c)
                        if prep and (t, c) == (0, 0):
                            route_in(tail[1])
                        if prep and (t, c) == (1, 0):
                            route_out(k + 1)
                        if prep and (t, c) == (3, 1):
                            take_comb(k + 1, tail[0] + COMB_AT[attn][0], tail[1] + COMB_AT[attn][1])
                        if attn:
                            attend_tail(k, at, tail, (t, c))
                        if isinstance(k, int) and k == 0 and c == 1 and 4 <= t < 4 + KC:
                            make_tables(t - 4)
                        if isinstance(k, int) and k == 0 and (t, c) == (6, 1):
                            split_attention_weights()
                s = s + TAIL
                out_copy(k, 0, at[1])
                if prep:
                    unit(s, 0, 0)
                out_copy(k, 1, at[1])
                add_to_x(fb, 0, out_at[0], out_at[1])
                if prep:
                    unit(s, 0, 1)
                add_to_x(fb, 1, out_at[0] + 1, out_at[1] + 1)
                dve.wait_ge(s0_used, out_at[0] + CHUNKS)
                dve.wait_ge(s1_used, out_at[1] + CHUNKS)

            def make_tables(m):
                linked(nc.vector.tensor_scalar(inv[:, m, :], half_scale[:, m, :], 1e-10, None, ALU.max))
                linked(nc.vector.reciprocal(inv[:, m, :], inv[:, m, :]))
                nc.vector.tensor_scalar(half_scale[:, m, :], half_scale[:, m, :], 0.5, None, ALU.mult).then_inc(table_done, 1)

            def split_attention_weights():
                dve.wait_ge(a_hi, 1)
                nc.vector.tensor_tensor(lo_a[:].rearrange("p w k n -> p (w k n)"), raw_a,
                                        hi_a[:].rearrange("p w k n -> p (w k n)").bitcast(F32), ALU.subtract).then_inc(a_lo, 1)
                dve.wait_ge(a_lo, 1)

            ROUTE_LINKS = 1 + 5 + 2 * TILES
            CHUNK_LINKS = {False: 2 * QUAD, True: 2 * QUAD + 2 * QUAD + 5 * KC}
            quiet = CHUNKS * CHUNK_LINKS[False] + ROUTE_LINKS
            busy = 1 + CHUNKS * CHUNK_LINKS[True] + ROUTE_LINKS + 1 + 2 + 2 * KC

            nc.vector.memset(ones[:], 1.0).then_inc(mem_set, 1)
            nc.vector.memset(mean_w[:], 1.0 / P).then_inc(mem_set, 1)
            nc.vector.memset(zero_f[:], 0.0).then_inc(mem_set, 1)
            dve.wait_ge(mem_set, 3)
            nc.vector.tensor_copy(zero_w[:], zero_f[:]).then_inc(mem_set, 1)
            dve.wait_ge(act_link, 1)
            nc.vector.tensor_scalar(par[:, 0, :], par[:, 0, :], 1e-7, None, ALU.max).then_inc(decay_done, 1)
            dve.wait_ge(x_in[0], GOLD)
            with counted_loop(dve, TILES, [link], [2]) as j:
                ffn_stats(j, j)
            with dve.Fori(0, TILES) as j:
                normalise(j, j, 1, ONE + j)
                low_z(0, j, j, ONE + j)
                take_logits(j, ONE + j)
            route_in(ONE + TILES)
            route_out(0)
            take_comb(0, ONE + TILES, ONE + TILES)
            for b in range(1, B):
                dve.wait_ge(x_in[b], GOLD)
            dve.wait_ge(consts_in[5], GOLD)
            dve.wait_ge(table_in, KC)
            unit(0, 0, 0)
            unit(0, 0, 1)
            walk(dve, block, [link], [quiet], [busy])

        @block_ctx.tensor
        def _(pe):
            hl_w, hl_z, hl_h = (hi_w, lo_w), (hi_z, lo_z), (hi_h, lo_h)
            hl_a, hl_za, hl_n = (hi_a, lo_a), (hi_za, lo_za), (hi_n, lo_n)

            def project(dst, weights, tokens):
                n = 0
                for kc in range(KC):
                    for a, b in FIRST_PRODUCTS:
                        mm = nc.tensor.matmul(dst, weights(a, kc), tokens(b, kc), start=(n == 0), stop=(n == 5))
                        n += 1
                return mm

            def gate_up(s, p, c, zp):
                u = s * UNITS + 2 * p + c
                if c == 0:
                    pe.wait_ge(w_split, s * SLOTS + p + 1 + SPLIT_CREDIT)
                tokens = lambda b, kc: hl_z[b][:, zp, kc, c * CH:(c + 1) * CH]
                pe.wait_ge(silu_done, u)
                project(G[:], lambda a, kc: hl_w[a][:, p, kc * P:(kc + 1) * P], tokens).then_inc(gate_done, 1)
                pe.wait_ge(gated, u)
                project(U[:], lambda a, kc: hl_w[a][:, p, (KC + kc) * P:(KC + kc + 1) * P], tokens).then_inc(up_done, 1)

            def down(s, p, c, last=False):
                u = s * UNITS + 2 * p + c
                pe.wait_ge(hidden, u + 1 + HIDDEN_CREDIT)
                for m in range(KC):
                    for i, (a, b) in enumerate(FIRST_PRODUCTS):
                        mm = nc.tensor.matmul(O[m][c][:], hl_w[a][:, p, 4 * P + m * P:4 * P + (m + 1) * P],
                                              hl_h[b][:, c, :], start=False, stop=(last and i == 2))
                mm.then_inc(down_done, 1)

            def clear(c):
                for m in range(KC):
                    nc.tensor.matmul(O[m][c][:], zero_w[:], hi_w[:, 0, 0:CH], start=True, stop=False)

            def transpose_tile(src, S, full, used, done, tile, at):
                pe.wait_ge(done, tile)
                pe.wait_ge(used, at)
                for kc in range(KC):
                    mm = nc.tensor.transpose(S[:, kc * P:(kc + 1) * P], src[:, kc * P:(kc + 1) * P], ident[:])
                mm.then_inc(full, 1)

            def route_logits(s0_at, s1_at):
                pe.wait_ge(s0_used, s0_at + 1)
                pe.wait_ge(s1_used, s1_at)
                for kc in range(KC):
                    mm = nc.tensor.matmul(S1[:, 0:COLS], zt[:, kc, :], router[:, kc, :], start=(kc == 0), stop=(kc == 1))
                mm.then_inc(s1_full, 1)

            def transpose_comb(k, s0_at, s1_at):
                pe.wait_ge(comb_done, k + 1)
                for full, used, S, at, h in ((s0_full, s0_used, S0, s0_at, 0), (s1_full, s1_used, S1, s1_at, 1)):
                    pe.wait_ge(used, at)
                    for t in range(QUAD):
                        mm = nc.tensor.transpose(S[0:COLS, t * P:(t + 1) * P], comb[:, h * QUAD + t, :], ident[:])
                    mm.then_inc(full, 1)

            def transpose_out(k, c, s0_at, s1_at):
                pe.wait_ge(out0_done, 2 * k + c + 1 + ONE)
                pe.wait_ge(out1_done, 2 * k + c + 1 + ONE)
                for full, used, S, at, g in ((s0_full, s0_used, S0, s0_at, 0), (s1_full, s1_used, S1, s1_at, 1)):
                    pe.wait_ge(used, at)
                    for t in range(2):
                        tok = c * CH + (g * 2 + t) * P
                        for m in range(KC):
                            mm = nc.tensor.transpose(S[:, t * D + m * P:t * D + (m + 1) * P],
                                                     ffn_o[:, m, tok:tok + P], ident[:])
                    mm.then_inc(full, 1)

            def attend(k, at, c, q):
                batch = k - 1
                if 2 <= q <= 5:
                    j = q - 2
                    which, use = A_AT[j]
                    transpose_tile(z_a, (S0, S1)[which], (s0_full, s1_full)[which], (s0_used, s1_used)[which],
                                   za_done, batch * TILES + c * QUAD + j + 1 + ONE, at[which] + use)
                for w, at_q, which, uses in ((1, (6, 8), 0, K_AT), (2, (6, 9), 1, V_AT), (0, (7, 10), 1, R_AT)):
                    if q in at_q:
                        m = at_q.index(q)
                        if w == 1:
                            pe.wait_ge(s0_used, at[0] + A_AT[3][1] + 1)
                            pe.wait_ge(s1_used, at[1] + A_AT[2][1] + 1)
                            pe.wait_ge(a_lo, 1)
                            if m:
                                pe.wait_ge(s1_used, at[1] + V_AT[0] + 1)
                        S, full, used = ((S0, s0_full, s0_used), (S1, s1_full, s1_used))[which]
                        pe.wait_ge(used, at[which] + uses[m])
                        project(S[:], lambda a, kc: hl_a[a][:, w, kc, m * P:(m + 1) * P],
                                lambda b, kc: hl_za[b][:, kc, :]).then_inc(full, 1)

            def attend_tail(k, tail, t):
                if t == 1:
                    pe.wait_ge(part_done, k)
                    pe.wait_ge(s1_used, tail[1] + MEAN_AT)
                    nc.tensor.matmul(S1[:, 0:1], mean_w[:], gstat[:, 0:1], start=True, stop=True).then_inc(s1_full, 1)
                if t == 2:
                    pe.wait_ge(spread_done, k)
                    pe.wait_ge(s1_used, tail[1] + VAR_AT)
                    nc.tensor.matmul(S1[:, 0:1], mean_w[:], gstat[:, 4:5], start=True, stop=True).then_inc(s1_full, 1)
                if t in (5, 7):
                    c = (t - 5) // 2
                    pe.wait_ge(n_split, 4 * (k - 1) + 2 * c + 2)
                    for which, (S, full, used) in enumerate(((S0, s0_full, s0_used), (S1, s1_full, s1_used))):
                        pe.wait_ge(used, tail[which] + WO_AT[which] + c)
                        for h in range(2):
                            tok = (2 * which + h) * P
                            mm = project(S[:, h * D:(h + 1) * D], lambda a, kc: hl_n[a][:, kc, tok:tok + P],
                                         lambda b, kc: hl_a[b][:, 3, kc, :])
                        mm.then_inc(full, 1)

            def block(k, fb, at, prep, attn):
                s, zp = k * STEPS, k % 2
                if prep:
                    with pe.Fori(0, CHUNKS) as c:
                        atc = [a + c * u for a, u in zip(at, QUAD_USES[attn])]
                        for i in range(QUAD):
                            j = c * QUAD + i
                            for p in range(SLOTS):
                                nxt = (s + j + (p + 1) // SLOTS, (p + 1) % SLOTS)
                                down(s + j, p, 0)
                                gate_up(*nxt, 0, zp)
                                down(s + j, p, 1)
                                f_at, l_at = atc[0] + F_AT[attn][i], atc[1] + L_AT[attn][i]
                                if p == 1:
                                    transpose_tile(z, S0, s0_full, s0_used, z_done, (k + 1) * TILES + j + 1, f_at)
                                if p == 2:
                                    route_logits(f_at, l_at)
                                if attn:
                                    attend(k, atc, c, i * SLOTS + p)
                                gate_up(*nxt, 1, zp)
                    tail = [a + CHUNKS * u for a, u in zip(at, QUAD_USES[attn])]
                    out_at = [a + u for a, u in zip(tail, OUT_AT[attn])]
                else:
                    with pe.Fori(0, TILES) as j:
                        for p in range(SLOTS):
                            nxt = (s + j + (p + 1) // SLOTS, (p + 1) % SLOTS)
                            for c in range(CHUNKS):
                                down(s + j, p, c)
                                gate_up(*nxt, c, zp)
                    out_at = at
                s = s + TILES
                for t in range(TAIL * SLOTS - 1):
                    i, p = divmod(t, SLOTS)
                    nxt = (s + (t + 1) // SLOTS, (t + 1) % SLOTS)
                    down(s + i, p, 0)
                    gate_up(*nxt, 0, zp)
                    down(s + i, p, 1)
                    if prep and t == 3:
                        transpose_comb(k + 1, tail[0] + COMB_AT[attn][0], tail[1] + COMB_AT[attn][1])
                    if attn:
                        attend_tail(k, tail, t)
                    gate_up(*nxt, 1, zp)
                s = s + TAIL - 1
                for c in range(CHUNKS):
                    down(s, SLOTS - 1, c, True)
                    if c == 0 and prep:
                        gate_up(s + 1, 0, 0, (k + 1) % 2)
                for c in range(CHUNKS):
                    transpose_out(k, c, out_at[0] + c, out_at[1] + c)
                    if prep:
                        clear(c)
                        if c == 0:
                            gate_up(s + 1, 0, 1, (k + 1) % 2)

            pe.wait_ge(consts_in[0], GOLD)
            pe.wait_ge(consts_in[1], GOLD)
            with pe.Fori(0, TILES) as j:
                transpose_tile(z, S0, s0_full, s0_used, z_done, j + 1, ONE + j)
                route_logits(ONE + j, ONE + j)
            transpose_comb(0, ONE + TILES, ONE + TILES)
            pe.wait_ge(mem_set, 4)
            gate_up(0, 0, 0, 0)
            clear(0)
            gate_up(0, 0, 1, 0)
            clear(1)
            walk(pe, block)


_INS = ["x", "w_pairs", "w_router", "w_attn", "decay", "gn", "eye", "pos"]
_OUT = ((4, 1024, 256), "float32")


def kernel(**inputs):
    import numpy as np
    import concourse.bacc as _bacc
    from concourse import mybir as _mybir
    from concourse.bass_utils import run_bass_kernel_spmd as _run

    a = {k: np.asarray(v) for k, v in inputs.items()}

    def f(name):
        return a["L0_ffn_" + name]

    gu = np.zeros((PAIRS * 2, 2, I, D), np.float32)
    gu[:E] = f("gate_up_proj").reshape(E, 2, I, D)
    gu[E, 0], gu[E, 1] = f("shared_gate_w"), f("shared_up_w")
    dn = np.zeros((PAIRS * 2, D, I), np.float32)
    dn[:E] = f("down_proj")
    dn[E] = f("shared_down_w")
    gu = gu.reshape(PAIRS, 2, 2, I, KC, P).transpose(0, 5, 2, 4, 1, 3).reshape(PAIRS, P, 4 * P)
    dn = dn.reshape(PAIRS, 2, D, I).transpose(0, 1, 3, 2).reshape(PAIRS, P, D)
    att = np.stack([a["L0_attn_" + n].T.reshape(KC, P, D) for n in ("Wr", "Wk", "Wv", "Wo")])
    arrays = {
        "x": a["L0_attn_x"],
        "w_pairs": np.concatenate([gu, dn], axis=2),
        "w_router": np.concatenate([f("router_w"), f("shared_expert_gate_w")]).T.reshape(KC, P, COLS).transpose(1, 0, 2),
        "w_attn": att.transpose(2, 0, 1, 3).reshape(P, 4 * KC * D),
        "decay": a["L0_attn_decay"].reshape(KC, P).T,
        "gn": np.stack([a["L0_attn_gn_weight"], a["L0_attn_gn_bias"]]).reshape(2, KC, P).transpose(2, 0, 1),
        "eye": np.eye(P, dtype=np.float32),
        "pos": np.arange(T, dtype=np.float32).reshape(1, T),
    }
    arrays = {f"in_{k}_dram": np.ascontiguousarray(arrays[k]) for k in _INS}
    nc = _bacc.Bacc("TRN2", target_bir_lowering=False, num_devices=1)
    args = [nc.dram_tensor(k, v.shape, _mybir.dt.from_np(v.dtype), kind="ExternalInput").ap() for k, v in arrays.items()]
    args.append(nc.dram_tensor("out_0_dram", _OUT[0], _mybir.dt.from_np(np.dtype(_OUT[1])), kind="ExternalOutput").ap())
    build(nc, *args)
    r = _run(nc, [arrays], core_ids=[0])
    return r.results[0]["out_0_dram"]
```

```python
from contextlib import ExitStack, contextmanager

import concourse.bass as bass
from concourse import mybir

F32 = mybir.dt.float32
F32R = mybir.dt.float32r
ALU = mybir.AluOpType
ACT = mybir.ActivationFunctionType
AX_X = mybir.AxisListType.X

P = 128
D = 256
KC = D // P
B, T = 4, 1024
TILES = T // P
CH = 512
CHUNKS = T // CH
E, I, TOPK = 64, 64, 8
COLS = E + 1
PAIRS = E // 2 + 1
SLOTS = 3
STEPS = PAIRS // SLOTS
PAIR_W = 4 * P + D
QUAD = TILES // CHUNKS
TAIL = STEPS - TILES
BLOCKS = 2 * B
EPS = 1e-5
GOLD = 16
FIRST_PRODUCTS = ((0, 0), (0, 1), (1, 0))
assert PAIRS == STEPS * SLOTS and TAIL == SLOTS

SPLIT_CREDIT = SLOTS
DOWN_CREDIT = 4
WEIGHTED_CREDIT = 2 * SLOTS
HIDDEN_CREDIT = 2
ONE = 1


class Count:

    def __init__(self, start=0):
        self.base, self.off = start, 0

    def at(self, more=0):
        return self.base + (self.off + more) if self.off + more else self.base

    def up(self):
        self.off += 1
        return self.at()


@contextmanager
def counted_loop(eng, times, counts, per):
    before = [(c.base, c.off) for c in counts]
    with eng.Fori(0, times) as i:
        for c, (base, off), k in zip(counts, before, per):
            c.base, c.off = base + i * k + off, 0
        yield i
        for c, k in zip(counts, per):
            assert c.off == k, (c.off, k)
    for c, (base, off), k in zip(counts, before, per):
        c.base, c.off = base, off + times * k


def build(nc, x, w_pairs, w_router, w_attn, decay, gn, eye, pos, out):
    with ExitStack() as ctx:
        def sb(name, shape, dt=F32):
            return ctx.enter_context(nc.sbuf_tensor(name, shape, dt))

        def bank(name):
            return ctx.enter_context(nc.psum_tensor(name, [P, CH], F32))

        def sem(name):
            return ctx.enter_context(nc.semaphore(name))

        X = sb("X", [P, B * TILES, D])
        raw_w = sb("raw_w", [P, SLOTS, PAIR_W])
        hi_w = sb("hi_w", [P, SLOTS, PAIR_W], F32R)
        lo_w = sb("lo_w", [P, SLOTS, PAIR_W], F32R)
        hi_z = sb("hi_z", [P, 2, KC, T], F32R)
        lo_z = sb("lo_z", [P, 2, KC, T], F32R)
        weight_b = sb("weight_b", [P, SLOTS, T])
        hid = sb("hid", [P, 2, CH])
        hi_h = sb("hi_h", [P, 2, CH], F32R)
        lo_h = sb("lo_h", [P, 2, CH], F32R)
        zero_f = sb("zero_f", [P, P])
        zero_w = sb("zero_w", [P, P], F32R)
        ffn_o = sb("ffn_o", [P, KC, T])
        z = sb("z", [P, D])
        zt = sb("zt", [P, KC, P])
        bn6 = sb("bn6", [P, 6])
        relay = sb("relay", [P, 1])
        mv = sb("mv", [P, 2])
        mean = sb("mean", [P, TILES])
        ve = sb("ve", [P, TILES])
        rstd = sb("rstd", [P, TILES])
        mhalf = sb("mhalf", [P, TILES])
        logit = sb("logit", [P, TILES, COLS])
        row_max = sb("row_max", [P, TILES])
        ex = sb("ex", [P, TILES, COLS])
        top = sb("top", [P, TILES, TOPK])
        rest = sb("rest", [P, TILES, E])
        tot = sb("tot", [P, TILES])
        rtot = sb("rtot", [P, TILES])
        comb = sb("comb", [P, TILES, COLS])
        comb_t = sb("comb_t", [COLS, T])
        ident = sb("ident", [P, P])
        router = sb("router", [P, KC, COLS])
        hi_a = sb("hi_a", [P, 4, KC, D], F32R)
        lo_a = sb("lo_a", [P, 4, KC, D], F32R)
        z_a = sb("z_a", [P, D])
        hi_za = sb("hi_za", [P, KC, CH], F32R)
        lo_za = sb("lo_za", [P, KC, CH], F32R)
        mean_a = sb("mean_a", [P, QUAD])
        ve_a = sb("ve_a", [P, QUAD])
        rstd_a = sb("rstd_a", [P, QUAD])
        r_s = sb("r_s", [P, CH])
        k_s = sb("k_s", [P, CH])
        carry = sb("carry", [P, KC])
        state = sb("state", [P, KC, T])
        half_scale = sb("half_scale", [P, KC, T])
        inv = sb("inv", [P, KC, T])
        hi_n = sb("hi_n", [P, KC, CH], F32R)
        lo_n = sb("lo_n", [P, KC, CH], F32R)
        ones = sb("ones", [P, 1])
        mean_w = sb("mean_w", [P, P])
        par = sb("par", [P, 3, KC])
        bn24 = sb("bn24", [P, 4, 6])
        gstat = sb("gstat", [P, 8])
        aff = sb("aff", [P, 2, KC])

        O = [[bank(f"O{m}{c}") for c in range(CHUNKS)] for m in range(KC)]
        G, U, S0, S1 = bank("G"), bank("U"), bank("S0"), bank("S1")
        comb_d = nc.dram_tensor("comb_scratch", (2, COLS, T), F32).ap()
        raw_a = state[:, :, :].rearrange("p k t -> p (k t)")
        pos_b = ffn_o[:, 0, :]
        first_z = state[:, :, :].rearrange("p k t -> p (k t)").rearrange("p (t c) -> p t c", c=D)
        first_zt = ffn_o
        first_banks = [G, U, O[0][0], O[0][1]]

        x_half = sem("x_half")
        x_in = [sem(f"x_in{b}") for b in range(B)]
        consts_in = [sem(f"consts_in{i}") for i in range(6)]
        w_in = [sem(f"w_in{i}") for i in range(SLOTS)]
        weight_in = [sem(f"weight_in{i}") for i in range(SLOTS)]
        w_hi, w_split = sem("w_hi"), sem("w_split")
        gate_done, up_done, down_done = sem("gate_done"), sem("up_done"), sem("down_done")
        silu_done, gated, weighted, hid_hi, hidden = (sem(n) for n in ("silu_done", "gated", "weighted", "hid_hi", "hidden"))
        out_done = sem("out_done")
        s0_full, s0_used, s1_full, s1_used = (sem(n) for n in ("s0_full", "s0_used", "s1_full", "s1_used"))
        first_full, first_zt_done, first_low = sem("first_full"), sem("first_zt_done"), sem("first_low")
        mean_done = sem("mean_done")
        var_done, rstd_done, z_done, z_hi = sem("var_done"), sem("rstd_done"), sem("z_done"), sem("z_hi")
        ex_in, ex_done, comb_done, comb_out = (sem(n) for n in ("ex_in", "ex_done", "comb_done", "comb_out"))
        dve_link, act_link = sem("dve_link"), sem("act_link")
        mem_set, exponent_set = sem("mem_set"), sem("exponent_set")
        var_a_done, rstd_a_done, za_done, za_hi = sem("var_a_done"), sem("rstd_a_done"), sem("za_done"), sem("za_hi")
        k_scaled = sem("k_scaled")
        part_done, spread_done, group_rstd, affine, normed, n_split = (
            sem(n) for n in ("part_done", "spread_done", "group_rstd", "affine", "normed", "n_split"))
        a_hi, a_lo, table_done, table_in, decay_done = sem("a_hi"), sem("a_lo"), sem("table_done"), sem("table_in"), sem("decay_done")
        stored, last_stored = sem("stored"), sem("last_stored")

        F_AT = {False: (0, 1, 2, 3), True: (0, 2, 5, 7)}
        L_AT = {False: (0, 1, 2, 3), True: (0, 3, 6, 9)}
        A_AT = ((0, 1), (1, 1), (1, 2), (0, 3))
        K_AT, V_AT, R_AT = (4, 6), (4, 7), (5, 8)
        QUAD_USES = {False: (4, 4), True: (8, 10)}
        COMB_AT = {False: (0, 0), True: (0, 2)}
        MEAN_AT, VAR_AT = 0, 1
        WO_AT = (1, 3)
        OUT_AT = {False: (1, 1), True: (3, 5)}
        USES = {a: tuple(CHUNKS * QUAD_USES[a][i] + OUT_AT[a][i] + CHUNKS for i in range(2)) for a in (False, True)}
        TABLE_PARTS = 8
        UNITS = 2 * SLOTS
        FIRST = (ONE + 2, ONE + 2)

        def walk(eng, block, counts=(), quiet=(), busy=()):
            at = FIRST
            block(0, 0, at, True, False)
            at = tuple(x + y for x, y in zip(at, USES[False]))
            with counted_loop(eng, B, list(counts), list(busy)) as b:
                block(b + 1, (b + 1) % B, tuple(x + b * y for x, y in zip(at, USES[True])), True, True)
            at = tuple(x + B * y for x, y in zip(at, USES[True]))
            with counted_loop(eng, 2, list(counts), list(quiet)) as b:
                block(b + B + 1, b + 1, tuple(x + b * y for x, y in zip(at, USES[False])), True, False)
            at = tuple(x + 2 * y for x, y in zip(at, USES[False]))
            block(BLOCKS - 1, B - 1, at, False, False)

        blk = nc.Block()
        block_ctx = ctx.enter_context(blk)

        @block_ctx.sync
        def _(sp):
            def load_w(pair, n, p):
                sp.wait_ge(w_split, n + 1)
                sp.dma_start(raw_w[:, p, :], w_pairs[pair]).then_inc(w_in[p], GOLD)

            def step(k, j, seam=False, final=False):
                s = k * STEPS + j
                for p in range(SLOTS):
                    n = s * SLOTS + p
                    if not (seam and p > 0):
                        load_w(j * SLOTS + p + 2, n + 2, (p + 2) % SLOTS)
                    elif not final:
                        load_w(p - 1, n + 2, p - 1)
                    if p == 0 and isinstance(j, int) and j == 0:
                        sp.wait_ge(comb_out, GOLD * (k + 1))
                    sp.wait_ge(weighted, 2 * n + 2)
                    for half in range(2):
                        e = E if (seam and p == SLOTS - 1) else (j * SLOTS + p) * 2 + half
                        sp.dma_start(weight_b[half * I:(half + 1) * I, p, :],
                                     comb_d[bass.ds(k % 2, 1), bass.ds(e, 1), :]
                                     .rearrange("o e t -> (o e) t").to_broadcast([I, T])).then_inc(weight_in[p], GOLD)

            def block(k, fb, at, prep, attn):
                step(k, 0)
                with sp.Fori(1, STEPS - 1) as j:
                    step(k, j)
                step(k, STEPS - 1, True, not prep)

            for h, done in enumerate((x_half, x_in[0])):
                sp.dma_start(X[:, h * QUAD:(h + 1) * QUAD, :],
                             x[0, h * CH:(h + 1) * CH, :].rearrange("(t p) c -> p t c", p=P)).then_inc(done, GOLD)
            sp.dma_start(par[:, 0, :], decay).then_inc(consts_in[4], GOLD)
            sp.dma_start(pos_b, pos.to_broadcast([P, T])).then_inc(consts_in[3], GOLD)
            sp.dma_start(ident[:], eye).then_inc(consts_in[0], GOLD)
            sp.dma_start(router[:], w_router).then_inc(consts_in[1], GOLD)
            load_w(0, 0, 0)
            load_w(1, 1, 1)
            sp.dma_start(par[:, 1:3, :], gn).then_inc(consts_in[5], GOLD)
            for b in range(1, B):
                sp.dma_start(X[:, b * TILES:(b + 1) * TILES, :],
                             x[b].rearrange("(t p) c -> p t c", p=P)).then_inc(x_in[b], GOLD)
            sp.wait_ge(first_full, len(first_banks))
            sp.dma_start(raw_a, w_attn).then_inc(consts_in[2], GOLD)
            walk(sp, block)
            end = tuple(f + 4 * a + 3 * n for f, a, n in zip(FIRST, USES[True], USES[False]))
            for c in range(CHUNKS):
                for g, used in enumerate((s0_used, s1_used)):
                    sp.wait_ge(used, end[g] + c + 1)
                    t = c * QUAD + g * 2
                    sp.dma_start(out[B - 1, t * P:(t + 2) * P, :].rearrange("(t p) c -> p t c", p=P),
                                 X[:, (B - 1) * TILES + t:(B - 1) * TILES + t + 2, :]).then_inc(last_stored, GOLD)
            sp.wait_ge(last_stored, 2 * CHUNKS * GOLD)

        @block_ctx.gpsimd
        def _(pool):
            pool.sem_inc(w_split, SPLIT_CREDIT)
            pool.sem_inc(down_done, DOWN_CREDIT)
            pool.sem_inc(weighted, WEIGHTED_CREDIT)
            pool.sem_inc(hidden, HIDDEN_CREDIT)
            for guard in (s0_full, s0_used, s1_full, s1_used, za_done):
                pool.sem_inc(guard, ONE)
            pool.memset(mhalf[:], -0.5).then_inc(exponent_set, 1)
            pool.wait_ge(exponent_set, 1)

            def split_lo(s, p):
                n = s * SLOTS + p
                pool.wait_ge(w_hi, n + 1)
                pool.tensor_tensor(lo_w[:, p, :], raw_w[:, p, :], hi_w[:, p, :].bitcast(F32),
                                   ALU.subtract).then_inc(w_split, 1)

            def rstd_of(j, n, tiles):
                pool.wait_ge(var_done, tiles)
                pool.tensor_tensor(rstd[:, bass.ds(j, n)], ve[:, bass.ds(j, n)], mhalf[:, 0:n], ALU.pow).then_inc(rstd_done, 1)

            def attend(k, at, c, q):
                batch = k - 1
                if q < QUAD:
                    pool.wait_ge(var_a_done, batch * TILES + c * QUAD + q + 1)
                    pool.tensor_tensor(rstd_a[:, q:q + 1], ve_a[:, q:q + 1], mhalf[:, 0:1], ALU.pow).then_inc(rstd_a_done, 1)
                if q in (6, 8):
                    m = (6, 8).index(q)
                    pool.wait_ge(s0_used, at[0] + K_AT[m] + 1)
                    pool.wait_ge(table_done, KC * TABLE_PARTS)
                    pool.tensor_tensor(k_s[:], k_s[:], inv[:, m, bass.ds(c * CH, CH)], ALU.mult).then_inc(k_scaled, 1)

            def block(k, fb, at, prep, attn):
                s = k * STEPS
                if prep:
                    with pool.Fori(0, CHUNKS) as c:
                        for i in range(QUAD):
                            for p in range(SLOTS):
                                q = i * SLOTS + p
                                split_lo(s + c * QUAD + i + (p + 2) // SLOTS, (p + 2) % SLOTS)
                                if p == 0:
                                    rstd_of(c * QUAD + i, 1, (k + 1) * TILES + c * QUAD + i + 1)
                                if attn:
                                    attend(k, [a + c * u for a, u in zip(at, QUAD_USES[True])], c, q)
                else:
                    with pool.Fori(0, TILES) as j:
                        for p in range(SLOTS):
                            split_lo(s + j + (p + 2) // SLOTS, (p + 2) % SLOTS)
                if not attn and not isinstance(k, int) or not prep:
                    store(fb - 1, at)
                for i in range(TAIL):
                    for p in range(SLOTS):
                        if prep or (i, p) < (TAIL - 1, 1):
                            split_lo(s + TILES + i + (p + 2) // SLOTS, (p + 2) % SLOTS)
                        if attn and (i, p) == (0, 2):
                            pool.wait_ge(s1_used, at[1] + CHUNKS * QUAD_USES[True][1] + VAR_AT + 1)
                            pool.tensor_tensor(gstat[:, 6:7], gstat[:, 5:6], mhalf[:, 0:1], ALU.pow).then_inc(group_rstd, 1)

            def store(b, at):
                pool.wait_ge(s0_used, at[0])
                pool.wait_ge(s1_used, at[1])
                pool.dma_start(out[bass.ds(b, 1), :, :].rearrange("o (t p) c -> p (o t) c", p=P),
                               X[:, bass.ds(b * TILES, TILES), :]).then_inc(stored, GOLD)

            rstd_of(0, TILES, TILES)
            split_lo(0, 0)
            split_lo(0, 1)
            walk(pool, block)
            pool.wait_ge(stored, (B - 1) * GOLD)

        @block_ctx.scalar
        def _(act):
            def split_hi(s, p):
                n = s * SLOTS + p
                act.wait_ge(w_in[p], GOLD * (s + 1))
                act.wait_ge(down_done, 2 * n)
                nc.scalar.activation(hi_w[:, p, :], raw_w[:, p, :], ACT.Copy).then_inc(w_hi, 1)

            def silu(s, p, c, shared=False):
                u = s * UNITS + 2 * p + c
                act.wait_ge(gate_done, u + 1)
                act.wait_ge(hidden, u + HIDDEN_CREDIT - 1)
                src, dst = (slice(0, I), slice(I, P)) if shared else (slice(0, P), slice(0, P))
                nc.scalar.activation(hid[dst, c, :], (U if shared and c else G)[src, :], ACT.Silu).then_inc(silu_done, 1)

            def high_z(zp, j, s0_at):
                act.wait_ge(s0_full, s0_at + 1)
                nc.scalar.activation(hi_z[:, zp, :, bass.ds(j * P, P)],
                                     S0[:, 0:D].rearrange("p (k t) -> p k t", k=KC), ACT.Copy).then_inc(z_hi, 1)

            def exps(k):
                act.wait_ge(ex_in, 2 * k + 2)
                nc.scalar.activation(ex[:], ex[:], ACT.Exp).then_inc(ex_done, 1)

            def store_comb(k, s0_at, s1_at):
                act.wait_ge(s0_used, s0_at + 1)
                act.wait_ge(s1_used, s1_at + 1)
                act.dma_start(comb_d[bass.ds(k % 2, 1)].rearrange("o e t -> (o e) t"), comb_t[:]).then_inc(comb_out, GOLD)

            def out_copy(k, c, s1_before):
                act.wait_ge(down_done, DOWN_CREDIT + 2 * PAIRS * (k + 1) - (1 - c))
                act.wait_ge(s1_full, s1_before)
                for m in range(KC):
                    nc.scalar.activation(ffn_o[:, m, c * CH:(c + 1) * CH], O[m][c][:], ACT.Copy, scale=0.5).then_inc(out_done, 1)

            def attend(k, at, c, q):
                batch = k - 1
                if 2 <= q <= 5:
                    j = q - 2
                    which, use = A_AT[j]
                    act.wait_ge((s0_full, s1_full)[which], at[which] + use + 1)
                    nc.scalar.activation(hi_za[:, :, j * P:(j + 1) * P],
                                         (S0, S1)[which][:, 0:D].rearrange("p (k t) -> p k t", k=KC),
                                         ACT.Copy).then_inc(za_hi, 1)
                if q in (6, 8):
                    m = (6, 8).index(q)
                    act.wait_ge(s0_full, at[0] + K_AT[m] + 1)
                    nc.scalar.activation(k_s[:], S0[:], ACT.Copy).then_inc(s0_used, 1)
                if q in (7, 10):
                    m = (7, 10).index(q)
                    act.wait_ge(s1_full, at[1] + R_AT[m] + 1)
                    nc.scalar.activation(r_s[:], S1[:], ACT.Tanh, scale=0.5).then_inc(s1_used, 1)

            def normalise_batch(c):
                for m in range(KC):
                    nc.scalar.activation(state[:, m, c * CH:(c + 1) * CH], state[:, m, c * CH:(c + 1) * CH], ACT.Identity,
                                         bias=aff[:, 1, m:m + 1], scale=aff[:, 0, m:m + 1]).then_inc(normed, 1)

            def attention_hi(w):
                act.wait_ge(consts_in[2], GOLD)
                nc.scalar.activation(hi_a[:, bass.ds(w, 1)].rearrange("p w k n -> p (w k n)"),
                                     raw_a[:, bass.ds(w * KC * D, KC * D)], ACT.Copy).then_inc(a_hi, 1)

            def pair(s, i, p, mid=None, shared=False):
                split_hi(s + (p + 2) // SLOTS, (p + 2) % SLOTS)
                nxt = (s + (p + 1) // SLOTS, (p + 1) % SLOTS)
                silu(*nxt, 0, shared)
                if mid:
                    mid()
                silu(*nxt, 1, shared)

            def block(k, fb, at, prep, attn):
                s = k * STEPS
                if prep:
                    with act.Fori(0, CHUNKS) as c:
                        atc = [a + c * u for a, u in zip(at, QUAD_USES[attn])]
                        for i in range(QUAD):
                            for p in range(SLOTS):
                                if isinstance(k, int) and k == 0 and p == 0 and i < 2:
                                    attention_hi(2 * c + i)

                                def mid():
                                    if p == 1:
                                        high_z((k + 1) % 2, c * QUAD + i, atc[0] + F_AT[attn][i])
                                    if attn:
                                        attend(k, atc, c, i * SLOTS + p)
                                pair(s + c * QUAD + i, i, p, mid)
                    tail = [a + CHUNKS * u for a, u in zip(at, QUAD_USES[attn])]
                else:
                    with act.Fori(0, TILES) as j:
                        for p in range(SLOTS):
                            pair(s + j, 0, p)
                s = s + TILES
                for i in range(TAIL):
                    for p in range(SLOTS):
                        if (i, p) == (TAIL - 1, SLOTS - 1):
                            break
                        if not prep and (i, p) == (TAIL - 1, 1):
                            silu(s + i, 2, 0, True)
                            silu(s + i, 2, 1, True)
                            break
                        pair(s + i, i, p, shared=(i, p) == (TAIL - 1, 1))
                        if prep and (i, p) == (0, 0):
                            exps(k + 1)
                        if prep and (i, p) == (1, 1):
                            store_comb(k + 1, tail[0] + COMB_AT[attn][0], tail[1] + COMB_AT[attn][1])
                        if attn and (i, p) == (1, 0):
                            act.wait_ge(affine, k)
                            normalise_batch(0)
                        if attn and (i, p) == (1, 1):
                            normalise_batch(1)
                s = s + TAIL - 1
                if prep:
                    split_hi(s + 1, 1)
                out_copy(k, 0, at[1])
                if prep:
                    silu(s + 1, 0, 0)
                out_copy(k, 1, at[1])
                if prep:
                    silu(s + 1, 0, 1)

            act.wait_ge(consts_in[4], GOLD)
            nc.scalar.activation(par[:, 0, :], par[:, 0, :], ACT.Sigmoid).then_inc(act_link, 1)
            act.wait_ge(decay_done, 1)
            nc.scalar.activation(par[:, 0, :], par[:, 0, :], ACT.Ln).then_inc(act_link, 1)
            act.wait_ge(act_link, 2)
            act.wait_ge(consts_in[3], GOLD)
            for m in range(KC):
                nc.scalar.activation(half_scale[:, m, :], pos_b, ACT.Exp, scale=par[:, 0, m:m + 1]).then_inc(table_in, 1)
            split_hi(0, 0)
            split_hi(0, 1)
            act.wait_ge(table_in, KC)
            for i, S in enumerate(first_banks):
                act.wait_ge(first_full, i + 1)
                for t in range(2):
                    src = S[:, t * D:(t + 1) * D].rearrange("p (k t) -> p k t", k=KC)
                    tok = slice((2 * i + t) * P, (2 * i + t + 1) * P)
                    nc.scalar.activation(first_zt[:, :, tok], src, ACT.Copy).then_inc(first_zt_done, 1)
                for t in range(2):
                    src = S[:, t * D:(t + 1) * D].rearrange("p (k t) -> p k t", k=KC)
                    tok = slice((2 * i + t) * P, (2 * i + t + 1) * P)
                    nc.scalar.activation(hi_z[:, 0, :, tok], src, ACT.Copy).then_inc(z_hi, 1)
            exps(0)
            silu(0, 0, 0)
            store_comb(0, ONE + 1, ONE + 1)
            silu(0, 0, 1)
            walk(act, block)

        @block_ctx.vector
        def _(dve):
            link = Count()

            def linked(ins):
                ins.then_inc(dve_link, 1)
                dve.wait_ge(dve_link, link.up())

            def stats(t, mean_to, ve_to, done):
                linked(nc.vector.bn_stats(bn6[:], X[:, bass.ds(t, 1), :].rearrange("p o c -> p (o c)")))
                nc.vector.tensor_copy(relay[:], bn6[:, 0:1])
                linked(nc.vector.bn_aggr(mv[:], bn6[:]))
                nc.vector.tensor_copy(mean_to, mv[:, 0:1]).then_inc(mean_done, 1)
                nc.vector.tensor_scalar(ve_to, mv[:, 1:2], EPS, None, ALU.add).then_inc(done, 1)

            def ffn_stats(t, j):
                stats(t, mean[:, bass.ds(j, 1)], ve[:, bass.ds(j, 1)], var_done)

            def normalise(t, j, rstd_at, s0_before):
                dve.wait_ge(rstd_done, rstd_at)
                dve.wait_ge(s0_full, s0_before)
                nc.vector.tensor_scalar(z[:], X[:, bass.ds(t, 1), :].rearrange("p o c -> p (o c)"), mean[:, bass.ds(j, 1)],
                                        rstd[:, bass.ds(j, 1)], ALU.subtract, ALU.mult).then_inc(z_done, 1)

            def low_z(zp, j, tile, s1_before):
                dve.wait_ge(z_hi, tile + 1)
                src = S0[:, 0:D].rearrange("p (k t) -> p k t", k=KC)
                nc.vector.tensor_tensor(lo_z[:, zp, :, bass.ds(j * P, P)], src,
                                        hi_z[:, zp, :, bass.ds(j * P, P)].bitcast(F32), ALU.subtract)
                dve.wait_ge(s1_full, s1_before)
                nc.vector.tensor_copy(zt[:], src).then_inc(s0_used, 1)

            def take_logits(j, s1_at):
                dve.wait_ge(s1_full, s1_at + 1)
                nc.vector.tensor_copy(logit[:, bass.ds(j, 1), :].rearrange("p o e -> p (o e)"),
                                      S1[:, 0:COLS]).then_inc(s1_used, 1)

            def route_in(s1_at):
                dve.wait_ge(s1_used, s1_at)
                linked(nc.vector.tensor_reduce(row_max[:], logit[:, :, 0:E], AX_X, ALU.max))
                nc.vector.tensor_tensor(ex[:, :, 0:E], logit[:, :, 0:E],
                                        row_max[:].rearrange("p (t o) -> p t o", o=1).to_broadcast([P, TILES, E]),
                                        ALU.subtract).then_inc(ex_in, 1)
                nc.vector.tensor_scalar(ex[:, :, E:COLS], logit[:, :, E:COLS], -1.0, None, ALU.mult).then_inc(ex_in, 1)

            def route_out(k, part):
                if part == 0:
                    dve.wait_ge(ex_done, k + 1)
                    linked(nc.vector.tensor_scalar(ex[:, :, E:COLS], ex[:, :, E:COLS], 1.0, None, ALU.add))
                    nc.vector.reciprocal(comb[:, :, E:COLS], ex[:, :, E:COLS]).then_inc(dve_link, 1)
                    link.up()
                if part in (0, 1):
                    for j in range(part * QUAD, (part + 1) * QUAD):
                        nc.vector.max(top[:, j, :], ex[:, j, 0:E]).then_inc(dve_link, 1)
                        link.up()
                if part == 1:
                    dve.wait_ge(dve_link, link.at())
                    nc.vector.tensor_reduce(tot[:], top[:], AX_X, ALU.add).then_inc(dve_link, 1)
                    link.up()
                if part == 2:
                    for j in range(TILES):
                        nc.vector.match_replace(rest[:, j, :], top[:, j, :], ex[:, j, 0:E], 0.0).then_inc(dve_link, 1)
                        link.up()
                if part == 3:
                    dve.wait_ge(dve_link, link.at())
                    linked(nc.vector.reciprocal(rtot[:], tot[:]))
                    linked(nc.vector.tensor_tensor(comb[:, :, 0:E], ex[:, :, 0:E], rest[:], ALU.subtract))
                    nc.vector.tensor_tensor(comb[:, :, 0:E], comb[:, :, 0:E],
                                            rtot[:].rearrange("p (t o) -> p t o", o=1).to_broadcast([P, TILES, E]),
                                            ALU.mult).then_inc(comb_done, 1)

            def take_comb(k, s0_at, s1_at):
                if not isinstance(k, int) or k > 0:
                    dve.wait_ge(comb_out, GOLD * k)
                for h, (full, used, S, at) in enumerate(((s0_full, s0_used, S0, s0_at), (s1_full, s1_used, S1, s1_at))):
                    dve.wait_ge(full, at + 1)
                    nc.vector.tensor_copy(comb_t[:, h * CH:(h + 1) * CH], S[0:COLS, :]).then_inc(used, 1)

            def unit(s, p, c, shared=False):
                u = s * UNITS + 2 * p + c
                rows = slice(I, P) if shared else slice(0, P)
                h, up, high = hid[rows, c, :], (G if shared and c == 0 else U)[rows, :], hi_h[rows, c, :]
                low = hi_h[0:I, c, :] if shared else lo_h[:, c, :]
                dve.wait_ge(up_done, u + 1)
                dve.wait_ge(silu_done, u + 1)
                nc.vector.tensor_tensor(h, h, up, ALU.mult).then_inc(gated, 1)
                dve.wait_ge(gated, u + 1)
                if c == 0:
                    dve.wait_ge(weight_in[p], 2 * GOLD * (s + 1))
                nc.vector.tensor_tensor(h, h, weight_b[rows, p, c * CH:(c + 1) * CH], ALU.mult).then_inc(weighted, 1)
                dve.wait_ge(weighted, u + 1 + WEIGHTED_CREDIT)
                dve.wait_ge(down_done, u + 3)
                nc.vector.tensor_copy(high, h).then_inc(hid_hi, 1)
                dve.wait_ge(hid_hi, u + 1)
                nc.vector.tensor_tensor(low, h, high.bitcast(F32), ALU.subtract).then_inc(hidden, 1)

            def add_to_x(b, c, at0, at1):
                for g, (full, used, S, at) in enumerate(((s0_full, s0_used, S0, at0), (s1_full, s1_used, S1, at1))):
                    xt = X[:, bass.ds(b * TILES + c * QUAD + g * 2, 2), :]
                    dve.wait_ge(full, at + 1)
                    nc.vector.tensor_tensor(xt, xt, S[:].rearrange("p (t c) -> p t c", t=2), ALU.add).then_inc(used, 1)

            def attend_x(k, at, c, q):
                batch = k - 1
                st = bass.ds(c * CH, CH)
                if q < QUAD:
                    stats(batch * TILES + c * QUAD + q, mean_a[:, q:q + 1], ve_a[:, q:q + 1], var_a_done)
                if q in (7, 10):
                    m = (7, 10).index(q)
                    dve.wait_ge(s1_used, at[1] + V_AT[m] + 1)
                    linked(nc.vector.tensor_tensor_scan(state[:, m, st], ones[:].to_broadcast([P, CH]), state[:, m, st],
                                                        carry[:, m:m + 1], ALU.mult, ALU.add))
                    linked(nc.vector.tensor_copy(carry[:, m:m + 1], state[:, m, bass.ds(c * CH + CH - 1, 1)]))
                if q in (8, 11):
                    m = (8, 11).index(q)
                    dve.wait_ge(s1_used, at[1] + R_AT[m] + 1)
                    linked(nc.vector.scalar_tensor_tensor(out=state[:, m, st], in0=r_s[:], scalar=1.0, in1=state[:, m, st],
                                                          op0=ALU.add, op1=ALU.mult))
                    linked(nc.vector.tensor_tensor(state[:, m, st], state[:, m, st], half_scale[:, m, st], ALU.mult))
                    linked(nc.vector.bn_stats(bn24[:, bass.ds(c * KC + m, 1), :].rearrange("p o s -> p (o s)"),
                                              state[:, m, st]))

            def attend_y(k, at, c, q):
                batch = k - 1
                tile = batch * TILES + c * QUAD
                if 2 <= q <= 5:
                    j = q - 2
                    which, use = A_AT[j]
                    dve.wait_ge(za_hi, tile + j + 1)
                    nc.vector.tensor_tensor(lo_za[:, :, j * P:(j + 1) * P],
                                            (S0, S1)[which][:, 0:D].rearrange("p (k t) -> p k t", k=KC),
                                            hi_za[:, :, j * P:(j + 1) * P].bitcast(F32),
                                            ALU.subtract).then_inc((s0_used, s1_used)[which], 1)
                if 1 <= q <= 4:
                    j = q - 1
                    dve.wait_ge(rstd_a_done, tile + j + 1)
                    if j:
                        which, use = A_AT[j - 1]
                        dve.wait_ge((s0_full, s1_full)[which], at[which] + use + 1)
                    nc.vector.tensor_scalar(z_a[:], X[:, bass.ds(tile + j, 1), :].rearrange("p o c -> p (o c)"),
                                            mean_a[:, j:j + 1], rstd_a[:, j:j + 1], ALU.subtract, ALU.mult).then_inc(za_done, 1)
                if q in (6, 9):
                    m = (6, 9).index(q)
                    dve.wait_ge(k_scaled, (batch * CHUNKS + c) * KC + m + 1)
                    dve.wait_ge(s1_full, at[1] + V_AT[m] + 1)
                    nc.vector.tensor_tensor(state[:, m, bass.ds(c * CH, CH)], k_s[:], S1[:], ALU.mult).then_inc(s1_used, 1)

            def split_n(c, m, k):
                dve.wait_ge(normed, 4 * (k - 1) + 2 * c + m + 1)
                src = state[:, m, c * CH:(c + 1) * CH]
                linked(nc.vector.tensor_copy(hi_n[:, m, :], src))
                nc.vector.tensor_tensor(lo_n[:, m, :], src, hi_n[:, m, :].bitcast(F32), ALU.subtract).then_inc(n_split, 1)

            def attend_tail(k, at, tail, pos):
                batch = k - 1
                if pos == (0, 1):
                    nc.vector.tensor_copy(relay[:], bn24[:, 0, 0:1])
                    nc.vector.bn_aggr(gstat[:, 0:2], bn24[:].rearrange("p a s -> p (a s)")).then_inc(part_done, 1)
                if pos == (1, 1):
                    dve.wait_ge(s1_full, tail[1] + MEAN_AT + 1)
                    nc.vector.tensor_copy(gstat[:, 2:3], S1[:, 0:1]).then_inc(s1_used, 1)
                    dve.wait_ge(s1_used, tail[1] + MEAN_AT + 1)
                    linked(nc.vector.tensor_tensor(gstat[:, 3:4], gstat[:, 0:1], gstat[:, 2:3], ALU.subtract))
                    nc.vector.tensor_scalar(gstat[:, 4:5], gstat[:, 3:4], gstat[:, 3:4], gstat[:, 1:2],
                                            ALU.mult, ALU.add).then_inc(spread_done, 1)
                if pos == (2, 1):
                    dve.wait_ge(s1_full, tail[1] + VAR_AT + 1)
                    nc.vector.tensor_scalar(gstat[:, 5:6], S1[:, 0:1], EPS, None, ALU.add).then_inc(s1_used, 1)
                if pos == (3, 0):
                    dve.wait_ge(group_rstd, k)
                    linked(nc.vector.tensor_scalar(aff[:, 0, :], par[:, 1, :], gstat[:, 6:7], None, ALU.mult))
                    linked(nc.vector.tensor_scalar(gstat[:, 6:8], aff[:, 0, :], gstat[:, 2:3], None, ALU.mult))
                    nc.vector.tensor_tensor(aff[:, 1, :], par[:, 2, :], gstat[:, 6:8], ALU.subtract).then_inc(affine, 1)
                if pos[0] in (4, 6):
                    split_n((pos[0] - 4) // 2, pos[1], k)
                if pos[0] in (5, 7) and pos[1] == 1:
                    c = (pos[0] - 5) // 2
                    add_to_x(batch, c, tail[0] + WO_AT[0] + c, tail[1] + WO_AT[1] + c)

            def block(k, fb, at, prep, attn):
                s = k * STEPS
                nb = (fb + 1) % B if isinstance(k, int) or attn else fb + 1
                first = isinstance(k, int) and k == 0
                if attn:
                    dve.wait_ge(a_lo, 4)
                    nc.vector.memset(carry[:], 0.0).then_inc(dve_link, 1)
                    link.up()
                if prep:
                    uses = QUAD_USES[attn]
                    with counted_loop(dve, CHUNKS, [link], [CHUNK_LINKS[attn] + (2 * TABLE_PARTS if first else 0)]) as c:
                        atc = [a + c * u for a, u in zip(at, uses)]
                        for i in range(QUAD):
                            j = c * QUAD + i
                            tile = (k + 1) * TILES + j
                            for p in range(SLOTS):
                                q = i * SLOTS + p
                                nxt = (s + j + (p + 1) // SLOTS, (p + 1) % SLOTS)
                                unit(*nxt, 0)
                                if p == 0:
                                    ffn_stats(nb * TILES + j, j)
                                if attn:
                                    attend_x(k, atc, c, q)
                                if first and p > 0:
                                    make_tables(c, i * 2 + p - 1)
                                unit(*nxt, 1)
                                if first and p == 0 and i >= 2:
                                    attention_lo(2 * c + i - 2)
                                if p == 0:
                                    normalise(nb * TILES + j, j, (k * TILES + j) + 2, atc[0] + F_AT[attn][i])
                                if p == 1:
                                    low_z((k + 1) % 2, j, tile, atc[1] + L_AT[attn][i])
                                if p == 2:
                                    take_logits(j, atc[1] + L_AT[attn][i])
                                if attn:
                                    attend_y(k, atc, c, q)
                    tail = [a + CHUNKS * u for a, u in zip(at, uses)]
                    out_at = [a + u for a, u in zip(tail, OUT_AT[attn])]
                else:
                    with dve.Fori(0, TILES) as j:
                        for p in range(SLOTS):
                            for c in range(CHUNKS):
                                unit(s + j + (p + 1) // SLOTS, (p + 1) % SLOTS, c)
                    out_at = at
                s = s + TILES
                for t in range(TAIL * SLOTS - 1):
                    nxt = (s + (t + 1) // SLOTS, (t + 1) % SLOTS)
                    for c in range(CHUNKS):
                        unit(*nxt, c, t == TAIL * SLOTS - 2)
                        if prep and (t, c) == (0, 0):
                            route_in(tail[1])
                        if prep and t in (1, 2):
                            route_out(k + 1, (t - 1) * CHUNKS + c)
                        if prep and (t, c) == (3, 1):
                            take_comb(k + 1, tail[0] + COMB_AT[attn][0], tail[1] + COMB_AT[attn][1])
                        if attn:
                            attend_tail(k, at, tail, (t, c))
                s = s + TAIL
                if prep:
                    unit(s, 0, 0)
                add_to_x(fb, 0, out_at[0], out_at[1])
                if prep:
                    unit(s, 0, 1)
                add_to_x(fb, 1, out_at[0] + 1, out_at[1] + 1)
                dve.wait_ge(s0_used, out_at[0] + CHUNKS)
                dve.wait_ge(s1_used, out_at[1] + CHUNKS)

            def make_tables(m, part):
                cols = slice(part * (T // TABLE_PARTS), (part + 1) * (T // TABLE_PARTS))
                scale, inverse = (a[:, bass.ds(m, 1), cols].rearrange("p o t -> p (o t)") for a in (half_scale, inv))
                linked(nc.vector.tensor_scalar(inverse, scale, 1e-10, None, ALU.max))
                nc.vector.tensor_copy(relay[:], ones[:])
                linked(nc.vector.reciprocal(inverse, inverse))
                nc.vector.tensor_scalar(scale, scale, 0.5, None, ALU.mult).then_inc(table_done, 1)

            def attention_lo(w):
                dve.wait_ge(a_hi, w + 1)
                nc.vector.tensor_tensor(lo_a[:, bass.ds(w, 1)].rearrange("p w k n -> p (w k n)"),
                                        raw_a[:, bass.ds(w * KC * D, KC * D)],
                                        hi_a[:, bass.ds(w, 1)].rearrange("p w k n -> p (w k n)").bitcast(F32),
                                        ALU.subtract).then_inc(a_lo, 1)

            ROUTE_LINKS = 1 + 5 + 2 * TILES
            CHUNK_LINKS = {False: 2 * QUAD, True: 2 * QUAD + 2 * QUAD + 5 * KC}
            quiet = CHUNKS * CHUNK_LINKS[False] + ROUTE_LINKS
            busy = 1 + CHUNKS * CHUNK_LINKS[True] + ROUTE_LINKS + 1 + 2 + 2 * KC

            nc.vector.memset(ones[:], 1.0).then_inc(mem_set, 1)
            nc.vector.memset(mean_w[:], 1.0 / P).then_inc(mem_set, 1)
            nc.vector.memset(zero_f[:], 0.0).then_inc(mem_set, 1)
            dve.wait_ge(mem_set, 3)
            nc.vector.tensor_copy(zero_w[:], zero_f[:]).then_inc(mem_set, 1)
            dve.wait_ge(act_link, 1)
            nc.vector.tensor_scalar(par[:, 0, :], par[:, 0, :], 1e-7, None, ALU.max).then_inc(decay_done, 1)
            for j in range(TILES):
                if j in (0, QUAD):
                    dve.wait_ge(x_in[0] if j else x_half, GOLD)
                nc.vector.bn_stats(top[:, j, 0:6], X[:, j, :]).then_inc(dve_link, 1)
                link.up()
            dve.wait_ge(dve_link, link.at())
            for j in range(TILES):
                nc.vector.bn_aggr(rest[:, j, 0:2], top[:, j, 0:6]).then_inc(dve_link, 1)
                link.up()
            dve.wait_ge(dve_link, link.at())
            nc.vector.tensor_scalar(ve[:].rearrange("p (t o) -> p t o", o=1), rest[:, :, 1:2], EPS, None,
                                    ALU.add).then_inc(var_done, TILES)
            nc.vector.tensor_copy(mean[:].rearrange("p (t o) -> p t o", o=1), rest[:, :, 0:1]).then_inc(mean_done, 1)
            dve.wait_ge(mean_done, 1)
            dve.wait_ge(rstd_done, 1)
            for j in range(TILES):
                nc.vector.tensor_scalar(first_z[:, j, :], X[:, j, :], mean[:, j:j + 1], rstd[:, j:j + 1],
                                        ALU.subtract, ALU.mult).then_inc(z_done, 1)
            for i, S in enumerate(first_banks):
                dve.wait_ge(z_hi, 2 * i + 2)
                for t in range(2):
                    tok = slice((2 * i + t) * P, (2 * i + t + 1) * P)
                    nc.vector.tensor_tensor(lo_z[:, 0, :, tok], S[:, t * D:(t + 1) * D].rearrange("p (k t) -> p k t", k=KC),
                                            hi_z[:, 0, :, tok].bitcast(F32), ALU.subtract).then_inc(first_low, 1)
            for h, (full, used, S) in enumerate(((s0_full, s0_used, S0), (s1_full, s1_used, S1))):
                dve.wait_ge(full, ONE + 1)
                nc.vector.tensor_copy(logit[:, h * QUAD:(h + 1) * QUAD, :],
                                      S[:, 0:QUAD * COLS].rearrange("p (t e) -> p t e", e=COLS)).then_inc(used, 1)
            route_in(ONE + 1)
            for part in range(4):
                route_out(0, part)
            take_comb(0, ONE + 1, ONE + 1)
            for b in range(1, B):
                dve.wait_ge(x_in[b], GOLD)
            dve.wait_ge(consts_in[5], GOLD)
            dve.wait_ge(table_in, KC)
            unit(0, 0, 0)
            unit(0, 0, 1)
            walk(dve, block, [link], [quiet], [busy])

        @block_ctx.tensor
        def _(pe):
            hl_w, hl_z, hl_h = (hi_w, lo_w), (hi_z, lo_z), (hi_h, lo_h)
            hl_a, hl_za, hl_n = (hi_a, lo_a), (hi_za, lo_za), (hi_n, lo_n)

            def project(dst, weights, tokens, before_last=None):
                n = 0
                for kc in range(KC):
                    for a, b in FIRST_PRODUCTS:
                        mm = nc.tensor.matmul(dst, weights(a, kc), tokens(b, kc), start=(n == 0), stop=(n == 5))
                        n += 1
                        if n == 5 and before_last is not None:
                            mm.then_inc(before_last, 1)
                return mm

            def gate_up(s, p, c, zp, shared=False, after_shared=False):
                u = s * UNITS + 2 * p + c
                if c == 0:
                    pe.wait_ge(w_split, s * SLOTS + p + 1 + SPLIT_CREDIT)
                tokens = lambda b, kc: hl_z[b][:, zp, kc, c * CH:(c + 1) * CH]
                gate = lambda a, kc: hl_w[a][:, p, kc * P:(kc + 1) * P]
                if shared:
                    if c == 0:
                        pe.wait_ge(silu_done, u)
                    else:
                        pe.wait_ge(gated, u - 1)
                    project((G, U)[c][:], gate, tokens, up_done).then_inc(gate_done, 1)
                    return
                if after_shared:
                    pe.wait_ge(gated, u - 1)
                else:
                    pe.wait_ge(silu_done, u)
                project(G[:], gate, tokens).then_inc(gate_done, 1)
                pe.wait_ge(gated, u)
                project(U[:], lambda a, kc: hl_w[a][:, p, (KC + kc) * P:(KC + kc + 1) * P], tokens).then_inc(up_done, 1)

            def down(s, p, c):
                u = s * UNITS + 2 * p + c
                pe.wait_ge(hidden, u + 1 + HIDDEN_CREDIT)
                for m in range(KC):
                    for a, b in FIRST_PRODUCTS:
                        mm = nc.tensor.matmul(O[m][c][:], hl_w[a][:, p, 4 * P + m * P:4 * P + (m + 1) * P],
                                              hl_h[b][:, c, :], start=False, stop=False)
                mm.then_inc(down_done, 1)

            def down_shared(s, c):
                p = SLOTS - 1
                pe.wait_ge(hidden, s * UNITS + 2 * p + c + 1 + HIDDEN_CREDIT)
                for m in range(KC):
                    cols = slice(4 * P + m * P, 4 * P + (m + 1) * P)
                    nc.tensor.matmul(O[m][c][:], hi_w[:, p, cols], hi_h[:, c, :], start=False, stop=False)
                    mm = nc.tensor.matmul(O[m][c][:], lo_w[I:P, p, cols], hi_h[I:P, c, :], start=False, stop=True)
                mm.then_inc(down_done, 1)

            def clear(c):
                for m in range(KC):
                    nc.tensor.matmul(O[m][c][:], zero_w[:], hi_w[:, 0, 0:CH], start=True, stop=False)

            def transpose_tile(src, S, full, used, done, tile, at):
                pe.wait_ge(done, tile)
                pe.wait_ge(used, at)
                for kc in range(KC):
                    mm = nc.tensor.transpose(S[:, kc * P:(kc + 1) * P], src[:, kc * P:(kc + 1) * P], ident[:])
                mm.then_inc(full, 1)

            def route_logits(s0_at, s1_at):
                pe.wait_ge(s0_used, s0_at + 1)
                pe.wait_ge(s1_used, s1_at)
                for kc in range(KC):
                    mm = nc.tensor.matmul(S1[:, 0:COLS], zt[:, kc, :], router[:, kc, :], start=(kc == 0), stop=(kc == 1))
                mm.then_inc(s1_full, 1)

            def transpose_comb(k, s0_at, s1_at):
                pe.wait_ge(comb_done, k + 1)
                for full, used, S, at, h in ((s0_full, s0_used, S0, s0_at, 0), (s1_full, s1_used, S1, s1_at, 1)):
                    pe.wait_ge(used, at)
                    for t in range(QUAD):
                        mm = nc.tensor.transpose(S[0:COLS, t * P:(t + 1) * P], comb[:, h * QUAD + t, :], ident[:])
                    mm.then_inc(full, 1)

            def transpose_out(k, c, s0_at, s1_at):
                pe.wait_ge(out_done, (2 * k + c + 1) * KC)
                for full, used, S, at, g in ((s0_full, s0_used, S0, s0_at, 0), (s1_full, s1_used, S1, s1_at, 1)):
                    pe.wait_ge(used, at)
                    for t in range(2):
                        tok = c * CH + (g * 2 + t) * P
                        for m in range(KC):
                            mm = nc.tensor.transpose(S[:, t * D + m * P:t * D + (m + 1) * P],
                                                     ffn_o[:, m, tok:tok + P], ident[:])
                    mm.then_inc(full, 1)

            def attend(k, at, c, q):
                batch = k - 1
                if 2 <= q <= 5:
                    j = q - 2
                    which, use = A_AT[j]
                    transpose_tile(z_a, (S0, S1)[which], (s0_full, s1_full)[which], (s0_used, s1_used)[which],
                                   za_done, batch * TILES + c * QUAD + j + 1 + ONE, at[which] + use)
                for w, at_q, which, uses in ((1, (6, 8), 0, K_AT), (2, (6, 9), 1, V_AT), (0, (7, 10), 1, R_AT)):
                    if q in at_q:
                        m = at_q.index(q)
                        if w == 1:
                            pe.wait_ge(s0_used, at[0] + A_AT[3][1] + 1)
                            pe.wait_ge(s1_used, at[1] + A_AT[2][1] + 1)
                            pe.wait_ge(a_lo, 4)
                            if m:
                                pe.wait_ge(s1_used, at[1] + V_AT[0] + 1)
                        S, full, used = ((S0, s0_full, s0_used), (S1, s1_full, s1_used))[which]
                        pe.wait_ge(used, at[which] + uses[m])
                        project(S[:], lambda a, kc: hl_a[a][:, w, kc, m * P:(m + 1) * P],
                                lambda b, kc: hl_za[b][:, kc, :]).then_inc(full, 1)

            def attend_tail(k, tail, t):
                if t == 1:
                    pe.wait_ge(part_done, k)
                    pe.wait_ge(s1_used, tail[1] + MEAN_AT)
                    nc.tensor.matmul(S1[:, 0:1], mean_w[:], gstat[:, 0:1], start=True, stop=True).then_inc(s1_full, 1)
                if t == 2:
                    pe.wait_ge(spread_done, k)
                    pe.wait_ge(s1_used, tail[1] + VAR_AT)
                    nc.tensor.matmul(S1[:, 0:1], mean_w[:], gstat[:, 4:5], start=True, stop=True).then_inc(s1_full, 1)
                if t in (5, 7):
                    c = (t - 5) // 2
                    pe.wait_ge(n_split, 4 * (k - 1) + 2 * c + 2)
                    for which, (S, full, used) in enumerate(((S0, s0_full, s0_used), (S1, s1_full, s1_used))):
                        pe.wait_ge(used, tail[which] + WO_AT[which] + c)
                        for h in range(2):
                            tok = (2 * which + h) * P
                            mm = project(S[:, h * D:(h + 1) * D], lambda a, kc: hl_n[a][:, kc, tok:tok + P],
                                         lambda b, kc: hl_a[b][:, 3, kc, :])
                        mm.then_inc(full, 1)

            def block(k, fb, at, prep, attn):
                s, zp = k * STEPS, k % 2
                if prep:
                    with pe.Fori(0, CHUNKS) as c:
                        atc = [a + c * u for a, u in zip(at, QUAD_USES[attn])]
                        for i in range(QUAD):
                            j = c * QUAD + i
                            for p in range(SLOTS):
                                nxt = (s + j + (p + 1) // SLOTS, (p + 1) % SLOTS)
                                down(s + j, p, 0)
                                gate_up(*nxt, 0, zp)
                                down(s + j, p, 1)
                                f_at, l_at = atc[0] + F_AT[attn][i], atc[1] + L_AT[attn][i]
                                if p == 1:
                                    transpose_tile(z, S0, s0_full, s0_used, z_done, (k + 1) * TILES + j + 1, f_at)
                                if p == 2:
                                    route_logits(f_at, l_at)
                                if attn:
                                    attend(k, atc, c, i * SLOTS + p)
                                gate_up(*nxt, 1, zp)
                    tail = [a + CHUNKS * u for a, u in zip(at, QUAD_USES[attn])]
                    out_at = [a + u for a, u in zip(tail, OUT_AT[attn])]
                else:
                    with pe.Fori(0, TILES) as j:
                        for p in range(SLOTS):
                            nxt = (s + j + (p + 1) // SLOTS, (p + 1) % SLOTS)
                            for c in range(CHUNKS):
                                down(s + j, p, c)
                                gate_up(*nxt, c, zp)
                    out_at = at
                s = s + TILES
                for t in range(TAIL * SLOTS - 1):
                    i, p = divmod(t, SLOTS)
                    nxt = (s + (t + 1) // SLOTS, (t + 1) % SLOTS)
                    shared = t == TAIL * SLOTS - 2
                    down(s + i, p, 0)
                    gate_up(*nxt, 0, zp, shared)
                    down(s + i, p, 1)
                    if prep and t == 3:
                        transpose_comb(k + 1, tail[0] + COMB_AT[attn][0], tail[1] + COMB_AT[attn][1])
                    if attn:
                        attend_tail(k, tail, t)
                    gate_up(*nxt, 1, zp, shared)
                s = s + TAIL - 1
                down_shared(s, 0)
                if prep:
                    gate_up(s + 1, 0, 0, (k + 1) % 2, after_shared=True)
                    down_shared(s, 1)
                    transpose_out(k, 0, out_at[0], out_at[1])
                    clear(0)
                    gate_up(s + 1, 0, 1, (k + 1) % 2)
                    transpose_out(k, 1, out_at[0] + 1, out_at[1] + 1)
                    clear(1)
                else:
                    transpose_out(k, 0, out_at[0], out_at[1])
                    down_shared(s, 1)
                    transpose_out(k, 1, out_at[0] + 1, out_at[1] + 1)

            pe.wait_ge(consts_in[0], GOLD)
            pe.wait_ge(consts_in[1], GOLD)
            for i, S in enumerate(first_banks):
                pe.wait_ge(z_done, 2 * i + 2)
                for t in range(2):
                    for kc in range(KC):
                        mm = nc.tensor.transpose(S[:, t * D + kc * P:t * D + (kc + 1) * P],
                                                 first_z[:, 2 * i + t, kc * P:(kc + 1) * P], ident[:])
                mm.then_inc(first_full, 1)
            for h, (full, S) in enumerate(((s0_full, S0), (s1_full, S1))):
                for t in range(QUAD):
                    j = h * QUAD + t
                    pe.wait_ge(first_zt_done, j + 1)
                    for kc in range(KC):
                        mm = nc.tensor.matmul(S[:, t * COLS:(t + 1) * COLS], first_zt[:, kc, j * P:(j + 1) * P],
                                              router[:, kc, :], start=(kc == 0), stop=(kc == 1))
                mm.then_inc(full, 1)
            pe.wait_ge(first_low, TILES)
            pe.wait_ge(mem_set, 4)
            gate_up(0, 0, 0, 0)
            clear(0)
            clear(1)
            transpose_comb(0, ONE + 1, ONE + 1)
            gate_up(0, 0, 1, 0)
            walk(pe, block)


_INS = ["x", "w_pairs", "w_router", "w_attn", "decay", "gn", "eye", "pos"]
_OUT = ((4, 1024, 256), "float32")


def kernel(**inputs):
    import numpy as np
    import concourse.bacc as _bacc
    from concourse import mybir as _mybir
    from concourse.bass_utils import run_bass_kernel_spmd as _run

    a = {k: np.asarray(v) for k, v in inputs.items()}

    def f(name):
        return a["L0_ffn_" + name]

    gu = np.zeros((PAIRS * 2, 2, I, D), np.float32)
    gu[:E] = f("gate_up_proj").reshape(E, 2, I, D)
    gu[E, 0], gu[E + 1, 0] = f("shared_gate_w"), f("shared_up_w")
    dn = np.zeros((PAIRS * 2, D, I), np.float32)
    dn[:E] = f("down_proj")
    dn[E] = dn[E + 1] = f("shared_down_w")
    gu = gu.reshape(PAIRS, 2, 2, I, KC, P).transpose(0, 5, 2, 4, 1, 3).reshape(PAIRS, P, 4 * P)
    dn = dn.reshape(PAIRS, 2, D, I).transpose(0, 1, 3, 2).reshape(PAIRS, P, D)
    att = np.stack([a["L0_attn_" + n].T.reshape(KC, P, D) for n in ("Wr", "Wk", "Wv", "Wo")])
    arrays = {
        "x": a["L0_attn_x"],
        "w_pairs": np.concatenate([gu, dn], axis=2),
        "w_router": np.concatenate([f("router_w"), f("shared_expert_gate_w")]).T.reshape(KC, P, COLS).transpose(1, 0, 2),
        "w_attn": att.transpose(2, 0, 1, 3).reshape(P, 4 * KC * D),
        "decay": a["L0_attn_decay"].reshape(KC, P).T,
        "gn": np.stack([a["L0_attn_gn_weight"], a["L0_attn_gn_bias"]]).reshape(2, KC, P).transpose(2, 0, 1),
        "eye": np.eye(P, dtype=np.float32),
        "pos": np.arange(T, dtype=np.float32).reshape(1, T),
    }
    arrays = {f"in_{k}_dram": np.ascontiguousarray(arrays[k]) for k in _INS}
    nc = _bacc.Bacc("TRN2", target_bir_lowering=False, num_devices=1)
    args = [nc.dram_tensor(k, v.shape, _mybir.dt.from_np(v.dtype), kind="ExternalInput").ap() for k, v in arrays.items()]
    args.append(nc.dram_tensor("out_0_dram", _OUT[0], _mybir.dt.from_np(np.dtype(_OUT[1])), kind="ExternalOutput").ap())
    build(nc, *args)
    r = _run(nc, [arrays], core_ids=[0])
    return r.results[0]["out_0_dram"]
```
